# Optimizing a Trainium2 kernel written in Bass

```python
import numpy as np
import jax
import jax.numpy as jnp

def _softmax(x, axis=-1):
    return jax.nn.softmax(x, axis=axis)

def _gelu(x):
    return jax.nn.gelu(x, approximate=True)

def _silu(x):
    return jax.nn.silu(x)

def _sigmoid(x):
    return jax.nn.sigmoid(x)

def _layernorm(x, axis=-1, eps=1e-05):
    m = jnp.mean(x, axis=axis, keepdims=True)
    v = jnp.var(x, axis=axis, keepdims=True)
    return (x - m) / jnp.sqrt(v + eps)

def _scatter_add(tgt, idx, src, axis=0):
    return tgt.at[idx].add(src)

def _segment_sum(src, seg, n):
    return jax.ops.segment_sum(src, seg, n)
kernel_name = 'mk_prb_d1_jaxref_r4_4858ad'

def setup_inputs(seed: int=0):
    np.random.seed(seed)
    _w = jnp.asarray

    def _L0_attn_setup():
        import jax, jax.numpy as jnp
        import numpy as np
        from jax import lax
        D_MODEL = 256
        B, T = (4, 512)
        LN_EPS = 1e-05

        def _ln(x, w, b):
            mu = jnp.mean(x, axis=-1, keepdims=True)
            var = jnp.mean((x - mu) ** 2, axis=-1, keepdims=True)
            return (x - mu) * lax.rsqrt(var + LN_EPS) * w + b

        def _wkv(u, k, v):
            Bb, Tt, C = k.shape

            def step(carry, kv):
                aa, bb = carry
                kk, vv = kv
                p = jnp.maximum(bb, u + kk)
                e1 = jnp.exp(bb - p)
                e2 = jnp.exp(u + kk - p)
                out = (e1 * aa + e2 * vv) / (e1 + e2)
                p2 = jnp.maximum(bb, kk)
                e1b = jnp.exp(bb - p2)
                e2b = jnp.exp(kk - p2)
                return ((e1b * aa + e2b * vv, p2 + jnp.log(e1b + e2b)), out)
            init = (jnp.zeros((Bb, C), k.dtype), jnp.zeros((Bb, C), k.dtype))
            _, outs = lax.scan(step, init, (jnp.swapaxes(k, 0, 1), jnp.swapaxes(v, 0, 1)))
            return jnp.swapaxes(outs, 0, 1)
        key = jax.random.key(seed)
        ks = jax.random.split(key, 12)
        C = D_MODEL
        s = 0.02
        return {'x': jax.random.normal(ks[0], (B, T, C), jnp.float32), 'time_decay': jax.random.normal(ks[1], (C,), jnp.float32), 'time_first': jax.random.normal(ks[2], (C,), jnp.float32) * 0.5, 'time_shift': jax.random.normal(ks[3], (1, 1, C), jnp.float32) * 0.1, 'Wk': jax.random.normal(ks[4], (C, C), jnp.float32) * s, 'Wv': jax.random.normal(ks[5], (C, C), jnp.float32) * s, 'Wr': jax.random.normal(ks[6], (C, C), jnp.float32) * s, 'Wck': jax.random.normal(ks[7], (4 * C, C), jnp.float32) * s, 'Wcv': jax.random.normal(ks[8], (C, 4 * C), jnp.float32) * s, 'Wcr': jax.random.normal(ks[9], (C, C), jnp.float32) * s, 'ln1_w': jnp.ones((C,), jnp.float32), 'ln1_b': jnp.zeros((C,), jnp.float32), 'ln2_w': jnp.ones((C,), jnp.float32), 'ln2_b': jnp.zeros((C,), jnp.float32)}
    _L0_attn_in = _L0_attn_setup()

    def _L0_ffn_setup():
        import jax, jax.numpy as jnp
        import numpy as np
        B, S, D = (4, 512, 256)
        O = 256
        E = 8
        K = 2
        key = jax.random.key(seed)
        k1, k2, k3, k4, k5 = jax.random.split(key, 5)
        scale = 1.0 / np.sqrt(D)
        x = jax.random.normal(k1, (B, S, D), dtype=jnp.float32)
        We = jax.random.uniform(k2, (E, D, O), dtype=jnp.float32, minval=-scale, maxval=scale)
        be = jax.random.uniform(k3, (E, O), dtype=jnp.float32, minval=-scale, maxval=scale)
        Wg = jax.random.uniform(k4, (D, E), dtype=jnp.float32, minval=-scale, maxval=scale)
        bg = jax.random.uniform(k5, (E,), dtype=jnp.float32, minval=-scale, maxval=scale)
        return {'x': x, 'We': We, 'be': be, 'Wg': Wg, 'bg': bg}
    _L0_ffn_in = _L0_ffn_setup()
    _d = {'L0_attn_x': _L0_attn_in['x'], 'L0_attn_time_decay': _L0_attn_in['time_decay'], 'L0_attn_time_first': _L0_attn_in['time_first'], 'L0_attn_time_shift': _L0_attn_in['time_shift'], 'L0_attn_Wk': _L0_attn_in['Wk'], 'L0_attn_Wv': _L0_attn_in['Wv'], 'L0_attn_Wr': _L0_attn_in['Wr'], 'L0_attn_Wck': _L0_attn_in['Wck'], 'L0_attn_Wcv': _L0_attn_in['Wcv'], 'L0_attn_Wcr': _L0_attn_in['Wcr'], 'L0_attn_ln1_w': _L0_attn_in['ln1_w'], 'L0_attn_ln1_b': _L0_attn_in['ln1_b'], 'L0_attn_ln2_w': _L0_attn_in['ln2_w'], 'L0_attn_ln2_b': _L0_attn_in['ln2_b'], 'L0_ffn_We': _L0_ffn_in['We'], 'L0_ffn_be': _L0_ffn_in['be'], 'L0_ffn_Wg': _L0_ffn_in['Wg'], 'L0_ffn_bg': _L0_ffn_in['bg']}
    _x0 = _d['L0_attn_x']
    _d['L0_attn_x'] = jax.random.normal(jax.random.fold_in(jax.random.key(seed), 1), (4, 1024, 256), dtype=_x0.dtype)
    del _x0
    return _d

def reference(L0_attn_x, L0_attn_time_decay, L0_attn_time_first, L0_attn_time_shift, L0_attn_Wk, L0_attn_Wv, L0_attn_Wr, L0_attn_Wck, L0_attn_Wcv, L0_attn_Wcr, L0_attn_ln1_w, L0_attn_ln1_b, L0_attn_ln2_w, L0_attn_ln2_b, L0_ffn_We, L0_ffn_be, L0_ffn_Wg, L0_ffn_bg):

    def _L0_attn_ref(x, time_decay, time_first, time_shift, Wk, Wv, Wr, Wck, Wcv, Wcr, ln1_w, ln1_b, ln2_w, ln2_b):
        import jax, jax.numpy as jnp
        import numpy as np
        from jax import lax
        D_MODEL = 256
        B, T = (4, 512)
        LN_EPS = 1e-05

        def _ln(x, w, b):
            mu = jnp.mean(x, axis=-1, keepdims=True)
            var = jnp.mean((x - mu) ** 2, axis=-1, keepdims=True)
            return (x - mu) * lax.rsqrt(var + LN_EPS) * w + b

        def _wkv(u, k, v):
            Bb, Tt, C = k.shape

            def step(carry, kv):
                aa, bb = carry
                kk, vv = kv
                p = jnp.maximum(bb, u + kk)
                e1 = jnp.exp(bb - p)
                e2 = jnp.exp(u + kk - p)
                out = (e1 * aa + e2 * vv) / (e1 + e2)
                p2 = jnp.maximum(bb, kk)
                e1b = jnp.exp(bb - p2)
                e2b = jnp.exp(kk - p2)
                return ((e1b * aa + e2b * vv, p2 + jnp.log(e1b + e2b)), out)
            init = (jnp.zeros((Bb, C), k.dtype), jnp.zeros((Bb, C), k.dtype))
            _, outs = lax.scan(step, init, (jnp.swapaxes(k, 0, 1), jnp.swapaxes(v, 0, 1)))
            return jnp.swapaxes(outs, 0, 1)
        Bb, Tt, C = x.shape
        ts = time_shift
        h = _ln(x, ln1_w, ln1_b)
        x_shifted = jnp.concatenate([jnp.broadcast_to(ts, (Bb, 1, C)), h[:, :-1, :]], axis=1)
        xxx = h + (h - x_shifted) * ts
        k = jnp.einsum('btc,oc->bto', xxx, Wk)
        v = jnp.einsum('btc,oc->bto', xxx, Wv)
        r = jax.nn.sigmoid(jnp.einsum('btc,oc->bto', xxx, Wr))
        wkv = _wkv(time_first, k, v)
        x = x + r * wkv
        h2 = _ln(x, ln2_w, ln2_b)
        xx2 = jnp.concatenate([h2[:, -1:, :], h2[:, :-1, :]], axis=1)
        xxx2 = h2 + (xx2 - h2) * ts
        kc = jnp.einsum('btc,oc->bto', xxx2, Wck)
        rc = jax.nn.sigmoid(jnp.einsum('btc,oc->bto', xxx2, Wcr))
        vv = jnp.einsum('bth,ch->btc', jax.nn.relu(kc) ** 2, Wcv)
        return x + rc * vv

    def _L0_ffn_ref(x, We, be, Wg, bg):
        import jax, jax.numpy as jnp
        import numpy as np
        B, S, D = (4, 512, 256)
        O = 256
        E = 8
        K = 2
        b, s, d = x.shape
        x_flat = x.reshape(-1, d)
        gates = jax.nn.softmax(x_flat @ Wg + bg, axis=-1)
        topk_gates, topk_idx = jax.lax.top_k(gates, K)
        topk_gates = topk_gates / jnp.sum(topk_gates, axis=1, keepdims=True)
        expert_out = jnp.einsum('nd,edo->neo', x_flat, We) + be
        selected = jnp.take_along_axis(expert_out, topk_idx[:, :, None], axis=1)
        out = jnp.sum(selected * topk_gates[:, :, None], axis=1)
        return out.reshape(b, s, -1)
    x = L0_attn_x
    xn = _layernorm(x, axis=-1)
    x = x + _L0_attn_ref(xn, L0_attn_time_decay, L0_attn_time_first, L0_attn_time_shift, L0_attn_Wk, L0_attn_Wv, L0_attn_Wr, L0_attn_Wck, L0_attn_Wcv, L0_attn_Wcr, L0_attn_ln1_w, L0_attn_ln1_b, L0_attn_ln2_w, L0_attn_ln2_b) + _L0_ffn_ref(xn, L0_ffn_We, L0_ffn_be, L0_ffn_Wg, L0_ffn_bg)
    return x

_drawn_inputs = setup_inputs


def setup_inputs(seed=0):
    import zlib

    import numpy as np

    out = dict(_drawn_inputs(seed))
    spreads = {'L0_attn_ln1_w': (1.0, 0.6),
     'L0_attn_ln1_b': (0.0, 0.1),
     'L0_attn_ln2_w': (1.0, 0.6),
     'L0_attn_ln2_b': (0.0, 0.8)}
    factors = {'L0_attn_time_first': 8.0,
     'L0_attn_time_shift': 7.43,
     'L0_attn_Wr': 3.085,
     'L0_attn_Wck': 2.697,
     'L0_attn_Wcr': 8.0,
     'L0_ffn_be': 4.377}
    for name, (base, spread) in spreads.items():
        noise = np.random.default_rng([zlib.crc32(name.encode()), seed]).standard_normal(out[name].shape)
        drawn = base * np.exp(spread * noise) if base else spread * noise
        out[name] = jnp.asarray(drawn.astype(out[name].dtype))
    for name, factor in factors.items():
        out[name] = (out[name] * factor).astype(out[name].dtype)
    return out
```

```python
import concourse.bass as bass
from concourse import mybir
from contextlib import ExitStack

P = 128
B = 4
T = 1024
C = 256
KC = C // P
U = 512
TU = U // P
NU = B * T // U
E = 8
HID = 4 * C
HB = HID // P
Q = E // 2
EPS = 1e-5

KVR0 = 0
WG0 = KVR0 + KC * 3 * C
WE0 = WG0 + KC * E
WCK0 = WE0 + KC * E * C
WCR0 = WCK0 + KC * HID
WCV0 = WCR0 + KC * C
WCOLS = WCV0 + HB * C
V_LN1W, V_LN1B, V_LN2W, V_LN2B, V_TS, V_U = (KC * i for i in range(6))
V_BG = 6 * KC
V_IOTA = V_BG + TU * E
V_ID = V_IOTA + TU * E
VCOLS = V_ID + P


def rwkv_moe(nc, x, weights, vectors, be, out):
    f32, f32r, u32 = mybir.dt.float32, mybir.dt.float32r, mybir.dt.uint32
    ALU, ACT = mybir.AluOpType, mybir.ActivationFunctionType
    x_u = x.rearrange("b (h t p) c -> (b h) p t c", h=T // U, p=P)
    out_u = out.rearrange("b (h t p) c -> (b h) p t c", h=T // U, p=P)

    with ExitStack() as ctx:
        def sb(name, shape, dt=f32):
            return ctx.enter_context(nc.sbuf_tensor(name, shape, dt))

        def sem(name):
            return ctx.enter_context(nc.semaphore(name))

        w_hi, w_lo = sb("w_hi", [P, WCV0], f32r), sb("w_lo", [P, WCV0], f32r)
        wcv_hi, wcv_lo = sb("wcv_hi", [P, WCOLS - WCV0], f32r), sb("wcv_lo", [P, WCOLS - WCV0], f32r)
        keep = sb("keep", [P, 2 * NU * TU * C])
        h2 = keep[:, 0:KC * NU * U].rearrange("p (k n) -> p k n", k=KC)
        z = keep[:, KC * NU * U:].rearrange("p (u n) -> p u n", u=NU)
        raw_a = keep[:, 0:KC * NU * U]
        RAW_A = KC * NU * U
        raw_b = keep[:, 2 * RAW_A - (WCOLS - RAW_A):2 * RAW_A]
        vec = sb("vec", [P, VCOLS])
        be_sb = sb("be_sb", [E, C])
        tsd = sb("tsd", [P, 3, KC])
        zero1 = sb("zero1", [P, 1])

        def v(col, kc=0):
            return vec[:, col + kc:col + kc + 1]
        ident = vec[:, V_ID:V_ID + P]
        iota = vec[:, V_IOTA:V_IOTA + TU * E].rearrange("p (t e) -> p t e", t=TU)
        bg = vec[:, V_BG:V_BG + TU * E].rearrange("p (t e) -> p t e", t=TU)

        xb = sb("xb", [P, TU * C])
        xn = sb("xn", [P, TU * C])
        nrm = sb("nrm", [P, TU * C])
        xnT_hi, xnT_lo = sb("xnT_hi", [P, KC, U], f32r), sb("xnT_lo", [P, KC, U], f32r)
        h = sb("h", [P, KC, U + 1])
        xx_hi, xx_lo = sb("xx_hi", [P, KC, U], f32r), sb("xx_lo", [P, KC, U], f32r)
        acc = sb("acc", [P, 2, TU * C])
        kg = sb("kg", [P, KC, U])
        vv = sb("vv", [P, KC, U])
        rr = sb("rr", [P, 2, KC, U])
        ep = sb("ep", [P, 2, KC, U])
        sl = sb("sl", [P, KC, U + 1])
        mm = sb("mm", [P, KC, U + 1])
        aa = sb("aa", [P, KC, U + 1])
        s_last = sb("s_last", [P, KC])
        st1, st2 = sb("st1", [P, TU, 6]), sb("st2", [P, TU, 6])
        mv1, mv2 = sb("mv1", [P, TU, 2]), sb("mv2", [P, TU, 2])
        ve1, r1, ve2, r2, nb1, s2, nb2, half_neg = (sb(n, [P, TU]) for n in (
            "ve1", "r1", "ve2", "r2", "nb1", "s2", "nb2", "half_neg"))
        ve3, r3, nb3 = (sb(n, [P, TU]) for n in ("ve3", "r3", "nb3"))
        lg, top = sb("lg", [P, TU, E]), sb("top", [P, TU, E])
        idx = sb("idx", [P, TU, E], u32)
        idxf = sb("idxf", [P, TU, 2])
        dif = sb("dif", [P, TU])
        tw = sb("tw", [P, 2, TU])
        hot = (lg, top)
        gate = sb("gate", [P, TU, E])
        gT = ep[0:E, 1, 0, :]

        bank = [ctx.enter_context(nc.psum_tensor(f"bank{i}", [P, U], f32)) for i in range(8)]
        XN_F, K_F, YT_F, BIAS_F, H2_F, HT_F = 0, 2, 8, 10, 12, 14
        moe_bank = bank[4:6]
        logit_bank, gT_bank = bank[6], bank[7]
        kc_bank, rc_bank = bank[4:6], bank[2:4]
        out_bank = [bank[6:8], bank[0:2]]

        vec_loaded, be_loaded = sem("vec_loaded"), sem("be_loaded")
        w_loaded = [sem(f"w_loaded{i}") for i in range(5)]
        hi_split, lo_split = sem("hi_split"), sem("lo_split")
        ts_ready, consts_ready = sem("ts_ready"), sem("consts_ready")
        x_loaded = sem("x_loaded")
        hT_done, xnT_done = sem("hT_done"), sem("xnT_done")
        kvr_done = sem("kvr_done")
        logits_done, gT_done = sem("logits_done"), sem("gT_done")
        bias_done = sem("bias_done")
        yT_done, h2T_done = sem("yT_done"), sem("h2T_done")
        moe_done = sem("moe_done")
        xnT_hi_ready, h_ready = sem("xnT_hi_ready"), sem("h_ready")
        kvr_read = sem("kvr_read")
        tw_ready, gT_ready = sem("tw_ready"), sem("gT_ready")
        eg_ready, ln_ready, ed_ready, sg_ready = (sem(n) for n in (
            "eg_ready", "ln_ready", "ed_ready", "sg_ready"))
        xx_hi_ready = sem("xx_hi_ready")
        h2_ready = sem("h2_ready")
        xnT_lo_ready = sem("xnT_lo_ready")
        logits_read, dif_ready, gates_own, gates_ready = (sem(n) for n in (
            "logits_read", "dif_ready", "gates_own", "gates_ready"))
        acc_init = sem("acc_init")
        moe_added = sem("moe_added")
        x1_ready = sem("x1_ready")
        ln2_own, ve3_ready, nrm2_ready = sem("ln2_own"), sem("ve3_ready"), sem("nrm2_ready")
        m_ready, ep_clipped, s_ready, d_ready, aa_ready = (sem(n) for n in (
            "m_ready", "ep_clipped", "s_ready", "d_ready", "aa_ready"))
        wkv_own = sem("wkv_own")
        ln1_own, ve1_ready, ve2_ready, nb2_ready = (sem(n) for n in (
            "ln1_own", "ve1_ready", "ve2_ready", "nb2_ready"))
        h_first = sem("h_first")
        xxx_ready, xx_lo_ready = sem("xxx_ready"), sem("xx_lo_ready")
        g_ready, r1_ready, r2_ready, r3_ready = (sem(n) for n in (
            "g_ready", "r1_ready", "r2_ready", "r3_ready"))
        xn_ready, nrm_ready, z_copied, z_ready = (sem(n) for n in (
            "xn_ready", "nrm_ready", "z_copied", "z_ready"))
        a_ready = sem("a_ready")
        ep_own, ts_own = sem("ep_own"), sem("ts_own")
        v_used, y_own, y_ready = sem("v_used"), sem("y_own"), sem("y_ready")
        x2_own = sem("x2_own")
        x2_hi_ready, x2_lo_ready = sem("x2_hi_ready"), sem("x2_lo_ready")
        kc_done, relu_ready, sq_ready, sq_hi_ready, sq_lo_ready, vv_done = (sem(n) for n in (
            "kc_done", "relu_ready", "sq_ready", "sq_hi_ready", "sq_lo_ready", "vv_done"))
        rc_done, rc_ready, rv_ready, out_ready, stored, out_read = (sem(n) for n in (
            "rc_done", "rc_ready", "rv_ready", "out_ready", "stored", "out_read"))

        CHUNKS = [(0, WE0), (WE0, WE0 + 2048), (WE0 + 2048, WCK0), (WCK0, RAW_A), (RAW_A, WCOLS)]

        def raw(a, b):
            return raw_a[:, a:b] if b <= RAW_A else raw_b[:, a - RAW_A:b - RAW_A]

        def parts(a, b):
            found = []
            if a < WCV0:
                e = min(b, WCV0)
                found.append((w_hi[:, a:e], w_lo[:, a:e], raw(a, e)))
            if b > WCV0:
                s = max(a, WCV0)
                found.append((wcv_hi[:, s - WCV0:b - WCV0], wcv_lo[:, s - WCV0:b - WCV0], raw(s, b)))
            return found
        N_SPLIT = [len(parts(a, b)) for a, b in CHUNKS]
        SPLIT = [sum(N_SPLIT[:i + 1]) for i in range(len(CHUNKS))]

        def from_zero(eng, semaphore, value):
            if not isinstance(value, int) or value > 0:
                eng.wait_ge(semaphore, value)

        def stand_alone(eng, *waits):
            values = [n if isinstance(n, int) else eng.to_reg(n) for _, n in waits]
            eng.wait_ge(vec_loaded, 16)
            for (semaphore, _), n in zip(waits, values):
                from_zero(eng, semaphore, n)

        block = ctx.enter_context(nc.Block())

        sq_hi = w_hi[:, WE0:WE0 + 4 * U].rearrange("p (s n) -> p s n", s=4)
        sq_lo = w_lo[:, WE0:WE0 + 4 * U].rearrange("p (s n) -> p s n", s=4)
        relu = acc[:, 0, :].rearrange("p (s n) -> p s n", s=2)
        sq = acc[:, 1, :].rearrange("p (s n) -> p s n", s=2)
        rc = xn
        xxx = nrm[:, :].rearrange("p (k n) -> p k n", k=KC)

        @block.sync
        def _(sp):
            sp.dma_start(xb[:, :].rearrange("p (t c) -> p t c", t=TU), x_u[0]).then_inc(x_loaded, 16)
            sp.dma_start(vec[:, :], vectors).then_inc(vec_loaded, 16)
            for i, (a, b) in enumerate(CHUNKS):
                sp.dma_start(raw(a, b), weights[:, a:b]).then_inc(w_loaded[i], 16)
                if i == 0:
                    sp.dma_start(be_sb[:, :], be).then_inc(be_loaded, 16)

            def load_x(u):
                sp.wait_ge(acc_init, 2 * u)
                sp.wait_ge(nrm_ready, u)
                sp.dma_start(xb[:, :].rearrange("p (t c) -> p t c", t=TU), x_u[u]).then_inc(x_loaded, 16)
            with sp.Fori(1, NU) as u:
                load_x(u)

            with sp.Fori(0, NU) as u:
                sp.wait_ge(out_ready, 2 * u + 2)
                sp.dma_start(out_u[u], z[:, u, :].rearrange("p (t c) -> p t c", t=TU)).then_inc(stored, 16)
            sp.wait_ge(stored, 16 * NU)

        @block.tensor
        def _(pe):
            mul = nc.tensor.matmul

            def wh(col, n=P):
                return w_hi[:, col:col + n]

            def wl(col, n=P):
                return w_lo[:, col:col + n]

            def h_transposes(u):
                pe.wait_ge(nrm_ready, u + 1)
                for k in range(KC):
                    from_zero(pe, acc_init, 2 * (u - 1) + k + 1)
                    for t in range(TU):
                        last = nc.tensor.transpose(bank[(HT_F + k) % 4][:, t * P:(t + 1) * P],
                                                   nrm[:, t * C + k * P:t * C + (k + 1) * P], ident)
                    last.then_inc(hT_done, 1)

            def xn_transposes(u):
                pe.wait_ge(xn_ready, u + 1)
                from_zero(pe, ln_ready, u)
                for k in range(KC):
                    for t in range(TU):
                        last = nc.tensor.transpose(bank[(XN_F + k) % 4][:, t * P:(t + 1) * P],
                                                   xn[:, t * C + k * P:t * C + (k + 1) * P], ident)
                    last.then_inc(xnT_done, 1)

            def project(u, i):
                if i == 0:
                    pe.wait_ge(xx_lo_ready, u + 1)
                    pe.wait_ge(xx_hi_ready, u + 1)
                    if isinstance(u, int) and u == 0:
                        pe.wait_ge(hi_split, SPLIT[0])
                        pe.wait_ge(lo_split, SPLIT[0])
                if i < 2:
                    pe.wait_ge(h_ready, 2 * u + i + 1)
                elif i < 4:
                    pe.wait_ge(xnT_lo_ready, 2 * u + i - 1)
                else:
                    pe.wait_ge(kvr_read, 6 * u + i - 3)
                ps = bank[(K_F + i) % 4]
                for k in range(KC):
                    col = KVR0 + k * 3 * C + i * P
                    mul(ps[:, :], wh(col), xx_hi[:, k, :], start=(k == 0), stop=False)
                    mul(ps[:, :], wh(col), xx_lo[:, k, :], start=False, stop=False)
                    last = mul(ps[:, :], wl(col), xx_hi[:, k, :], start=False, stop=(k == KC - 1))
                last.then_inc(kvr_done, 1)

            def logits(u):
                pe.wait_ge(xnT_lo_ready, 2 * u + 2)
                pe.wait_ge(xnT_hi_ready, 2 * u + 2)
                from_zero(pe, logits_read, u)
                for t in range(TU):
                    ps = logit_bank[:, t * E:(t + 1) * E]
                    ts = slice(t * P, (t + 1) * P)
                    for k in range(KC):
                        col = WG0 + k * E
                        mul(ps, xnT_hi[:, k, ts], wh(col, E), start=(k == 0), stop=False)
                        mul(ps, xnT_hi[:, k, ts], wl(col, E), start=False, stop=False)
                        last = mul(ps, xnT_lo[:, k, ts], wh(col, E), start=False, stop=(k == KC - 1))
                last.then_inc(logits_done, 1)

            def y_transposes(u):
                pe.wait_ge(y_ready, u + 1)
                for i in range(2):
                    if isinstance(u, int) and u == NU - 1:
                        pe.wait_ge(h2_ready, 2 * u)
                    else:
                        pe.wait_ge(kvr_read, 6 * (u + 1) + 2 + i + 1)
                    for t in (2 * i, 2 * i + 1):
                        for k in range(KC):
                            at = (t % 2) * C + k * P
                            last = nc.tensor.transpose(bank[(YT_F + i) % 4][:, at:at + P],
                                                       ep[:, 0, k, t * P:(t + 1) * P], ident)
                    last.then_inc(yT_done, 1)

            def h2_transposes(u):
                pe.wait_ge(nrm2_ready, 4 * u + 4)
                for k in range(KC):
                    pe.wait_ge(x1_ready, 2 * u + k + 1)
                    for t in range(TU):
                        last = nc.tensor.transpose(bank[(H2_F + k) % 4][:, t * P:(t + 1) * P],
                                                   nrm[:, t * C + k * P:t * C + (k + 1) * P], ident)
                    last.then_inc(h2T_done, 1)

            def gate_bias(u):
                pe.wait_ge(gates_ready, u + 1)
                from_zero(pe, gT_ready, u)
                for t in range(TU):
                    last = nc.tensor.transpose(gT_bank[0:E, t * P:(t + 1) * P], gate[:, t, :], ident)
                last.then_inc(gT_done, 1)
                pe.wait_ge(gT_ready, u + 1)
                for i in range(2):
                    pe.wait_ge(kvr_read, 6 * u + 4 + i + 1)
                    for t in (2 * i, 2 * i + 1):
                        last = mul(bank[(BIAS_F + i) % 4][:, (t % 2) * C:(t % 2 + 1) * C],
                                   gT[:, t * P:(t + 1) * P], be_sb[:, :], start=True, stop=True)
                    last.then_inc(bias_done, 1)

            def experts(u, f):
                t, q = f // Q, f % Q
                from_zero(pe, moe_added, 32 * u + 2 * (f - 1))
                ps = moe_bank[f % 2]
                ts = slice(t * P, (t + 1) * P)
                for k in range(KC):
                    col = WE0 + k * E * C + q * 2 * C
                    mul(ps[:, :], xnT_hi[:, k, ts], wh(col, 2 * C), start=(k == 0), stop=False)
                    mul(ps[:, :], xnT_hi[:, k, ts], wl(col, 2 * C), start=False, stop=False)
                    last = mul(ps[:, :], xnT_lo[:, k, ts], wh(col, 2 * C), start=False, stop=(k == KC - 1))
                last.then_inc(moe_done, 1)

            def step(u, first=False, last=False):
                xn_transposes(u)
                for i in range(4):
                    project(u, i)
                logits(u)
                project(u, 4)
                project(u, 5)
                if not first:
                    y_transposes(u - 1)
                gate_bias(u)
                if first:
                    pe.wait_ge(hi_split, SPLIT[2])
                    pe.wait_ge(lo_split, SPLIT[2])
                for f in range(TU * Q):
                    experts(u, f)
                    if f == 3 and not first:
                        h2_transposes(u - 1)
                    if f == 9 and not last:
                        h_transposes(u + 1)

            pe.wait_ge(vec_loaded, 16)
            pe.wait_ge(be_loaded, 16)
            h_transposes(0)
            step(0, first=True)
            with pe.Fori(0, (NU - 2) // 2) as i:
                step(2 * i + 1)
                step(2 * i + 2)
            step(NU - 1, last=True)
            y_transposes(NU - 1)
            h2_transposes(NU - 1)

            x2_hi, x2_lo = (xx_hi, xnT_hi), (xx_lo, xnT_lo)

            def hidden(u, par, j):
                if j == 0:
                    pe.wait_ge(x2_lo_ready, u + 1)
                    pe.wait_ge(x2_hi_ready, u + 1)
                from_zero(pe, relu_ready, HB * u + j - 1)
                ps = kc_bank[j % 2]
                for k in range(KC):
                    col = WCK0 + k * HID + j * P
                    mul(ps[:, :], wh(col), x2_hi[par][:, k, :], start=(k == 0), stop=False)
                    mul(ps[:, :], wh(col), x2_lo[par][:, k, :], start=False, stop=False)
                    last = mul(ps[:, :], wl(col), x2_hi[par][:, k, :], start=False, stop=(k == KC - 1))
                last.then_inc(kc_done, 1)

            def receptance(u, par, i):
                from_zero(pe, rc_ready, 2 * u + i - 1)
                for t in (2 * i, 2 * i + 1):
                    ps = rc_bank[i][:, (t % 2) * C:(t % 2 + 1) * C]
                    ts = slice(t * P, (t + 1) * P)
                    for k in range(KC):
                        col = WCR0 + k * C
                        mul(ps, x2_hi[par][:, k, ts], wh(col, C), start=(k == 0), stop=False)
                        mul(ps, x2_hi[par][:, k, ts], wl(col, C), start=False, stop=False)
                        last = mul(ps, x2_lo[par][:, k, ts], wh(col, C), start=False, stop=(k == KC - 1))
                last.then_inc(rc_done, 1)

            def values(u, par, j):
                pe.wait_ge(sq_lo_ready, HB * u + j + 1)
                pe.wait_ge(sq_hi_ready, HB * u + j + 1)
                if j == 0:
                    from_zero(pe, rv_ready, 2 * (u - 1))
                hi, lo = sq_hi[:, j % 4, :], sq_lo[:, j % 4, :]
                for t in range(TU):
                    ps = out_bank[par][t // 2][:, (t % 2) * C:(t % 2 + 1) * C]
                    ts = slice(t * P, (t + 1) * P)
                    col = slice(j * C, (j + 1) * C)
                    mul(ps, hi[:, ts], wcv_hi[:, col], start=(j == 0 and t % 2 == 0), stop=False,
                        skip_group_check=True)
                    mul(ps, hi[:, ts], wcv_lo[:, col], start=False, stop=False, skip_group_check=True)
                    last = mul(ps, lo[:, ts], wcv_hi[:, col], start=False, stop=(j == HB - 1),
                               skip_group_check=True)
                last.then_inc(vv_done, 1)

            def mix(u, par):
                for j in range(HB):
                    hidden(u, par, j)
                    if j >= 2:
                        values(u, par, j - 2)
                receptance(u, par, 0)
                values(u, par, HB - 2)
                receptance(u, par, 1)
                values(u, par, HB - 1)

            pe.wait_ge(hi_split, SPLIT[4])
            pe.wait_ge(lo_split, SPLIT[4])
            pe.wait_ge(h2_ready, 2 * NU)
            mix(0, 0)
            mix(1, 1)
            with pe.Fori(1, NU // 2) as i:
                mix(2 * i, 0)
                mix(2 * i + 1, 1)

        @block.scalar
        def _(act):
            act_fn = nc.scalar.activation

            def split_hi(i):
                act.wait_ge(w_loaded[i], 16)
                for hi, _, src in parts(*CHUNKS[i]):
                    act_fn(hi, src, ACT.Copy).then_inc(hi_split, 1)

            def h_read(u):
                act.wait_ge(h_first, u + 1)
                for k in range(KC):
                    act.wait_ge(hT_done, 2 * u + k + 1)
                    act_fn(h[:, k, 1:U + 1], bank[(HT_F + k) % 4][:, :], ACT.Identity,
                           bias=v(V_LN1B, k), scale=v(V_LN1W, k)).then_inc(h_ready, 1)

            def xx_split(u):
                act.wait_ge(xxx_ready, 2 * u + 2)
                from_zero(act, kvr_done, 6 * u)
                act_fn(xx_hi[:, :, :], xxx, ACT.Copy).then_inc(xx_hi_ready, 1)

            def xn_read(u):
                for k in range(KC):
                    act.wait_ge(xnT_done, 2 * u + k + 1)
                    act_fn(xnT_hi[:, k, :], bank[(XN_F + k) % 4][:, :], ACT.Copy).then_inc(xnT_hi_ready, 1)

            def kvr(u, par, lo, hi):
                for i in range(lo, hi):
                    act.wait_ge(kvr_done, 6 * u + i + 1)
                    if i == 0:
                        from_zero(act, d_ready, u)
                        from_zero(act, sg_ready, 2 * u)
                    if i == 2:
                        from_zero(act, v_used, u)
                    if i == 4:
                        from_zero(act, g_ready, u)
                    ps = bank[(K_F + i) % 4][:, :]
                    if i < 4:
                        act_fn((kg, vv)[i // 2][:, i % 2, :], ps, ACT.Copy).then_inc(kvr_read, 1)
                    else:
                        act_fn(rr[:, par, i % 2, :], ps, ACT.Sigmoid).then_inc(kvr_read, 1)

            def top_weights(u):
                act.wait_ge(dif_ready, u + 1)
                act_fn(tw[:, 0, :], dif[:, :], ACT.Sigmoid).then_inc(tw_ready, 1)
                act_fn(tw[:, 1, :], dif[:, :], ACT.Sigmoid, scale=-1.0).then_inc(tw_ready, 1)

            def gT_read(u):
                act.wait_ge(gT_done, u + 1)
                from_zero(act, y_ready, u)
                act_fn(gT, gT_bank[0:E, :], ACT.Copy).then_inc(gT_ready, 1)

            def exp_g(u):
                act.wait_ge(g_ready, u + 1)
                from_zero(act, yT_done, 2 * u)
                act.wait_ge(bias_done, 2 * u + 2)
                act_fn(ep[:, 0], kg[:, :, :], ACT.Exp).then_inc(eg_ready, 1)
                act_fn(ep[:, 1], kg[:, :, :], ACT.Exp, scale=-1.0).then_inc(eg_ready, 1)

            def ln_s(u):
                act.wait_ge(s_ready, u + 1)
                act_fn(sl[:, :, 1:U + 1], sl[:, :, 1:U + 1], ACT.Ln).then_inc(ln_ready, 1)

            def exp_d(u):
                act.wait_ge(d_ready, u + 1)
                act_fn(ep[:, 0], kg[:, :, :], ACT.Exp).then_inc(ed_ready, 1)
                act_fn(ep[:, 1], kg[:, :, :], ACT.Exp, scale=-1.0).then_inc(ed_ready, 1)

            def sigmoid_d(u):
                act.wait_ge(aa_ready, 2 * u + 2)
                for k in range(KC):
                    act_fn(ep[:, 1, k, :], kg[:, k, :], ACT.Sigmoid, bias=v(V_U, k)).then_inc(sg_ready, 1)

            def h2_read(u):
                for k in range(KC):
                    act.wait_ge(h2T_done, 2 * u + k + 1)
                    act_fn(h2[:, k, u * U:(u + 1) * U] if isinstance(u, int) else h2[:, k, bass.ds(u * U, U)],
                           bank[(H2_F + k) % 4][:, :], ACT.Identity,
                           bias=v(V_LN2B, k), scale=v(V_LN2W, k)).then_inc(h2_ready, 1)

            def step(u, par, first=False, last=False):
                xn_read(u)
                kvr(u, par, 0, 4)
                top_weights(u)
                kvr(u, par, 4, 6)
                gT_read(u)
                if first:
                    split_hi(1)
                    split_hi(2)
                exp_g(u)
                if first:
                    split_hi(3)
                    split_hi(4)
                if not first:
                    h2_read(u - 1)
                ln_s(u)
                exp_d(u)
                if not last:
                    h_read(u + 1)
                sigmoid_d(u)
                if not last:
                    xx_split(u + 1)

            act.wait_ge(vec_loaded, 16)
            split_hi(0)
            h_read(0)
            xx_split(0)
            step(0, 0, first=True)
            act.wait_ge(lo_split, SPLIT[4])
            with act.Fori(0, (NU - 2) // 2) as i:
                step(2 * i + 1, 1)
                step(2 * i + 2, 0)
            step(NU - 1, 1, last=True)
            h2_read(NU - 1)

            x2_hi = (xx_hi, xnT_hi)

            def x2_split(u, par):
                act.wait_ge(x2_own, 3 * KC * (u + 1))
                from_zero(act, kc_done, HB * (u - 1))
                from_zero(act, rc_done, 2 * (u - 1))
                act_fn(x2_hi[par][:, :, :], xxx, ACT.Copy).then_inc(x2_hi_ready, 1)

            def mix(u, par, last=False):
                for j in range(HB):
                    act.wait_ge(kc_done, HB * u + j + 1)
                    from_zero(act, sq_ready, HB * u + j - 1)
                    act_fn(relu[:, j % 2, :], kc_bank[j % 2][:, :], ACT.Relu).then_inc(relu_ready, 1)
                    act.wait_ge(relu_ready, HB * u + j + 1)
                    from_zero(act, sq_lo_ready, HB * u + j - 1)
                    from_zero(act, sq_hi_ready, HB * u + j - 1)
                    act_fn(sq[:, j % 2, :], relu[:, j % 2, :], ACT.Square).then_inc(sq_ready, 1)
                    if j == 4 and not last:
                        x2_split(u + 1, 1 - par)
                for i in range(2):
                    act.wait_ge(rc_done, 2 * u + i + 1)
                    from_zero(act, out_ready, 2 * u + i - 1)
                    act_fn(rc[:, i * 2 * C:(i + 1) * 2 * C], rc_bank[i][:, :],
                           ACT.Sigmoid).then_inc(rc_ready, 1)

            x2_split(0, 0)
            act.wait_ge(z_ready, NU)
            mix(0, 0)
            mix(1, 1)
            with act.Fori(1, NU // 2 - 1) as i:
                mix(2 * i, 0)
                mix(2 * i + 1, 1)
            mix(NU - 2, 0)
            mix(NU - 1, 1, last=True)

        @block.vector
        def _(dve):
            tt, ts_, stt = nc.vector.tensor_tensor, nc.vector.tensor_scalar, nc.vector.scalar_tensor_tensor
            scan = nc.vector.tensor_tensor_scan
            copy = nc.vector.tensor_copy

            def tile(buf, t, n=1):
                return buf[:, t * C:(t + n) * C]

            def split_lo(i):
                dve.wait_ge(hi_split, SPLIT[i])
                for hi, lo, src in parts(*CHUNKS[i]):
                    tt(lo, src, hi, ALU.subtract).then_inc(lo_split, 1)

            def ln1_stats(u):
                dve.wait_ge(x_loaded, 16 * (u + 1))
                for t in range(TU):
                    nc.vector.bn_stats(st1[:, t, :], tile(xb, t)).then_inc(ln1_own, 1)
                stand_alone(dve, (ln1_own, 10 * u + 4))
                for t in range(TU):
                    nc.vector.bn_aggr(mv1[:, t, :], st1[:, t, :]).then_inc(ln1_own, 1)
                dve.wait_ge(ln1_own, 10 * u + 8)
                ts_(ve1[:, :], mv1[:, :, 1], EPS, None, ALU.add).then_inc(ve1_ready, 1)

            def ln1_inner(u):
                dve.wait_ge(r1_ready, u + 1)
                tt(ve2[:, :], r1[:, :], r1[:, :], ALU.mult).then_inc(ln1_own, 1)
                dve.wait_ge(ln1_own, 10 * u + 9)
                tt(ve2[:, :], ve2[:, :], mv1[:, :, 1], ALU.mult).then_inc(ln1_own, 1)
                dve.wait_ge(ln1_own, 10 * u + 10)
                ts_(ve2[:, :], ve2[:, :], EPS, None, ALU.add).then_inc(ve2_ready, 1)

            def ln1_coefficients(u):
                from_zero(dve, nrm_ready, u)
                stt(nb1[:, :], mv1[:, :, 0], -1.0, r1[:, :], ALU.mult, ALU.mult).then_inc(nb2_ready, 1)
                dve.wait_ge(r2_ready, u + 1)
                tt(s2[:, :], r1[:, :], r2[:, :], ALU.mult).then_inc(nb2_ready, 1)
                dve.wait_ge(nb2_ready, 3 * u + 2)
                tt(nb2[:, :], nb1[:, :], r2[:, :], ALU.mult).then_inc(nb2_ready, 1)

            def h_column(start):
                if start:
                    copy(h[:, :, 0], vec[:, V_TS:V_TS + KC]).then_inc(h_first, 1)
                else:
                    copy(h[:, :, 0], h[:, :, U]).then_inc(h_first, 1)

            def xxx_mix(u, next_starts, last=False):
                for k in range(KC):
                    dve.wait_ge(a_ready, 2 * u + k + 1)
                    stt(xxx[:, k, :], h[:, k, 0:U], tsd[:, 1, k:k + 1], xxx[:, k, :],
                        ALU.mult, ALU.add).then_inc(xxx_ready, 1)
                if not last:
                    dve.wait_ge(xxx_ready, 2 * u + 2)
                    h_column(next_starts)

            def xx_low(u):
                dve.wait_ge(xx_hi_ready, u + 1)
                tt(xx_lo[:, :, :], xxx, xx_hi[:, :, :], ALU.subtract).then_inc(xx_lo_ready, 1)

            def xn_low(u):
                for k in range(KC):
                    dve.wait_ge(xnT_hi_ready, 2 * u + k + 1)
                    tt(xnT_lo[:, k, :], bank[(XN_F + k) % 4][:, :], xnT_hi[:, k, :],
                       ALU.subtract).then_inc(xnT_lo_ready, 1)

            def gates(u):
                dve.wait_ge(logits_done, u + 1)
                tt(lg[:, :, :], logit_bank[:, 0:TU * E].rearrange("p (t e) -> p t e", t=TU), bg,
                   ALU.add).then_inc(logits_read, 1)
                stand_alone(dve, (logits_read, u + 1))
                for t in range(TU):
                    nc.vector.max(top[:, t, :], lg[:, t, :]).then_inc(gates_own, 1)
                dve.wait_ge(gates_own, 13 * u + 4)
                tt(dif[:, :], top[:, :, 0], top[:, :, 1], ALU.subtract).then_inc(dif_ready, 1)
                for t in range(TU):
                    nc.vector.max_index(idx[:, t, :], top[:, t, :], lg[:, t, :]).then_inc(gates_own, 1)
                dve.wait_ge(gates_own, 13 * u + 8)
                copy(idxf[:, :, :], idx[:, :, 0:2]).then_inc(gates_own, 1)
                dve.wait_ge(gates_own, 13 * u + 9)
                for n in range(2):
                    tt(hot[n][:, :, :], iota, idxf[:, :, n:n + 1].to_broadcast([P, TU, E]),
                       ALU.is_equal).then_inc(gates_own, 1)
                dve.wait_ge(gates_own, 13 * u + 11)
                dve.wait_ge(tw_ready, 2 * u + 2)
                for n in range(2):
                    tt(hot[n][:, :, :], hot[n][:, :, :], tw[:, n, :].unsqueeze(2).to_broadcast([P, TU, E]),
                       ALU.mult).then_inc(gates_own, 1)
                dve.wait_ge(gates_own, 13 * u + 13)
                tt(gate[:, :, :], hot[0][:, :, :], hot[1][:, :, :], ALU.add).then_inc(gates_ready, 1)

            def start_acc(u, par):
                dve.wait_ge(z_copied, u + 1)
                for i in range(2):
                    dve.wait_ge(bias_done, 2 * u + i + 1)
                    tt(tile(acc[:, par], 2 * i, 2), tile(xb, 2 * i, 2), bank[(BIAS_F + i) % 4][:, :],
                       ALU.add).then_inc(acc_init, 1)

            def add_experts(u, par, f0, f1):
                for f in range(f0, f1):
                    t, q = f // Q, f % Q
                    if f == 0:
                        dve.wait_ge(acc_init, 2 * u + 2)
                    dve.wait_ge(moe_done, TU * Q * u + f + 1)
                    for n in range(2):
                        dve.wait_ge(moe_added, 32 * u + 2 * f + n)
                        a = tile(acc[:, par], t)
                        stt(a, moe_bank[f % 2][:, n * C:(n + 1) * C], gate[:, t, 2 * q + n:2 * q + n + 1], a,
                            ALU.mult, ALU.add).then_inc(moe_added, 1)

            def add_y(u):
                dve.wait_ge(z_copied, u + 1)
                for i in range(2):
                    dve.wait_ge(yT_done, 2 * u + i + 1)
                    zi = z[:, u, 2 * i * C:2 * (i + 1) * C]
                    tt(zi, zi, bank[(YT_F + i) % 4][:, :], ALU.add).then_inc(x1_ready, 1)

            def ln2_stats(u):
                stand_alone(dve, (x1_ready, 2 * u + 2))
                for t in range(TU):
                    nc.vector.bn_stats(st2[:, t, :], z[:, u, t * C:(t + 1) * C]).then_inc(ln2_own, 1)
                stand_alone(dve, (ln2_own, 9 * u + 4))
                for t in range(TU):
                    nc.vector.bn_aggr(mv2[:, t, :], st2[:, t, :]).then_inc(ln2_own, 1)
                dve.wait_ge(ln2_own, 9 * u + 8)
                ts_(ve3[:, :], mv2[:, :, 1], EPS, None, ALU.add).then_inc(ve3_ready, 1)

            def ln2_norm(u):
                dve.wait_ge(r3_ready, u + 1)
                stt(nb3[:, :], mv2[:, :, 0], -1.0, r3[:, :], ALU.mult, ALU.mult).then_inc(ln2_own, 1)
                dve.wait_ge(ln2_own, 9 * u + 9)
                from_last = min(u + 2, NU) if isinstance(u, int) else u + 2
                dve.wait_ge(xx_lo_ready, from_last)
                dve.wait_ge(xx_hi_ready, from_last)
                for t in range(TU):
                    ts_(tile(nrm, t), z[:, u, t * C:(t + 1) * C], r3[:, t:t + 1], nb3[:, t:t + 1],
                        ALU.mult, ALU.add).then_inc(nrm2_ready, 1)

            def wkv_max(u, start):
                from_zero(dve, g_ready, u)
                if start:
                    nc.vector.memset(mm[:, :, 0], 0.0).then_inc(wkv_own, 1)
                else:
                    copy(mm[:, :, 0], mm[:, :, U]).then_inc(wkv_own, 1)
                dve.wait_ge(wkv_own, 4 * u + 1)
                for k in range(KC):
                    dve.wait_ge(kvr_read, 6 * u + k + 1)
                    scan(mm[:, k, 1:U + 1], kg[:, k, :], zero1[:, 0:1].to_broadcast([P, U]),
                         mm[:, k, 0:1], ALU.max, ALU.max).then_inc(m_ready, 1)

            def wkv_clip(u):
                dve.wait_ge(eg_ready, 2 * u + 2)
                ts_(ep[:, :, :, :], ep[:, :, :, :], 1.0, None, ALU.min).then_inc(ep_clipped, 1)
                dve.wait_ge(ep_clipped, u + 1)

            def wkv_sum(u, start):
                if start:
                    nc.vector.memset(sl[:, :, 0], 0.0).then_inc(wkv_own, 1)
                    nc.vector.memset(s_last[:, :], 1.0).then_inc(wkv_own, 1)
                else:
                    copy(sl[:, :, 0], sl[:, :, U]).then_inc(wkv_own, 2)
                dve.wait_ge(wkv_own, 4 * u + 3)
                for k in range(KC):
                    scan(sl[:, k, 1:U + 1], ep[:, 1, k, :], ep[:, 0, k, :], s_last[:, k:k + 1],
                         ALU.mult, ALU.add).then_inc(m_ready, 1)
                dve.wait_ge(m_ready, 4 * u + 4)
                copy(s_last[:, :], sl[:, :, U]).then_inc(s_ready, 1)

            def wkv_d(u):
                dve.wait_ge(ln_ready, u + 1)
                tt(kg[:, :, :], kg[:, :, :], sl[:, :, 0:U], ALU.subtract).then_inc(d_ready, 1)

            def wkv_coefficients(u, start):
                dve.wait_ge(ed_ready, 2 * u + 2)
                ts_(ep[:, 1], ep[:, 1], 1.0, None, ALU.min).then_inc(ep_own, 1)
                stt(ep[:, 0], ep[:, 0], 1.0, vv[:, :, :], ALU.min, ALU.mult).then_inc(ep_own, 1)
                from_zero(dve, y_ready, u)
                if start:
                    nc.vector.memset(aa[:, :, 0], 0.0).then_inc(wkv_own, 1)
                else:
                    copy(aa[:, :, 0], aa[:, :, U]).then_inc(wkv_own, 1)

            def wkv_aa(u):
                dve.wait_ge(ep_own, 2 * u + 2)
                dve.wait_ge(wkv_own, 4 * u + 4)
                for k in range(KC):
                    scan(aa[:, k, 1:U + 1], ep[:, 1, k, :], ep[:, 0, k, :], aa[:, k, 0:1],
                         ALU.mult, ALU.add).then_inc(aa_ready, 1)

            def step(u, par, start, first=False, last=False):
                xn_low(u)
                gates(u)
                wkv_max(u, start)
                if first:
                    split_lo(1)
                if not first:
                    add_y(u - 1)
                start_acc(u, par)
                if first:
                    split_lo(2)
                if not first:
                    ln2_stats(u - 1)
                add_experts(u, par, 0, 2)
                if not first:
                    ln2_norm(u - 1)
                add_experts(u, par, 2, 3)
                wkv_clip(u)
                add_experts(u, par, 3, 4)
                wkv_sum(u, start)
                if not last:
                    ln1_stats(u + 1)
                add_experts(u, par, 4, 6)
                if not last:
                    ln1_inner(u + 1)
                wkv_d(u)
                add_experts(u, par, 6, 7)
                if not last:
                    ln1_coefficients(u + 1)
                add_experts(u, par, 7, 9)
                wkv_coefficients(u, start)
                add_experts(u, par, 9, 10)
                wkv_aa(u)
                add_experts(u, par, 10, 12)
                if not last:
                    xxx_mix(u + 1, next_starts=start, last=(isinstance(u, int) and u == NU - 2))
                add_experts(u, par, 12, 14)
                if not last:
                    xx_low(u + 1)
                if first:
                    split_lo(3)
                    split_lo(4)
                add_experts(u, par, 14, 16)

            nc.vector.memset(zero1[:, :], 0.0).then_inc(ts_own, 1)
            nc.vector.memset(half_neg[:, :], -0.5).then_inc(consts_ready, 1)
            ln1_stats(0)
            dve.wait_ge(vec_loaded, 16)
            ts_row = vec[:, V_TS:V_TS + KC]
            ts_(tsd[:, 0, :], ts_row, 1.0, None, ALU.add).then_inc(ts_ready, 1)
            ts_(tsd[:, 1, :], ts_row, -1.0, None, ALU.mult).then_inc(ts_ready, 1)
            ts_(tsd[:, 2, :], ts_row, -1.0, 1.0, ALU.mult, ALU.add).then_inc(ts_ready, 1)
            h_column(True)
            ln1_inner(0)
            ln1_coefficients(0)
            split_lo(0)
            dve.wait_ge(ts_ready, 3)
            dve.wait_ge(ts_own, 1)
            xxx_mix(0, next_starts=False)
            xx_low(0)
            step(0, 0, True, first=True)
            with dve.Fori(0, (NU - 2) // 2) as i:
                step(2 * i + 1, 1, False)
                step(2 * i + 2, 0, True)
            step(NU - 1, 1, False, last=True)
            add_y(NU - 1)
            ln2_stats(NU - 1)
            ln2_norm(NU - 1)

            x2_hi, x2_lo = (xx_hi, xnT_hi), (xx_lo, xnT_lo)

            def x2_mix(u, half):
                dve.wait_ge(h2_ready, 2 * NU)
                from_zero(dve, x2_hi_ready, u)
                for k in range(KC):
                    ts_(xxx[:, k, :], h2[:, k, bass.ds(u * U, U)], tsd[:, 2, k:k + 1], None,
                        ALU.mult).then_inc(x2_own, 1)
                for k in range(KC):
                    dve.wait_ge(x2_own, 3 * KC * u + k + 1)
                    ts_k = v(V_TS, k)
                    if half == 0:
                        stt(xxx[:, k, 1:U], h2[:, k, bass.ds(u * U, U - 1)], ts_k, xxx[:, k, 1:U],
                            ALU.mult, ALU.add).then_inc(x2_own, 1)
                        stt(xxx[:, k, 0:1], h2[:, k, bass.ds(u * U + T - 1, 1)], ts_k, xxx[:, k, 0:1],
                            ALU.mult, ALU.add).then_inc(x2_own, 1)
                    else:
                        stt(xxx[:, k, :], h2[:, k, bass.ds(u * U - 1, U)], ts_k, xxx[:, k, :],
                            ALU.mult, ALU.add).then_inc(x2_own, 2)

            def x2_low(u, par):
                dve.wait_ge(x2_hi_ready, u + 1)
                tt(x2_lo[par][:, :, :], xxx, x2_hi[par][:, :, :], ALU.subtract).then_inc(x2_lo_ready, 1)

            def squares(u, j):
                dve.wait_ge(sq_ready, HB * u + j + 1)
                from_zero(dve, vv_done, HB * u + j - 3)
                copy(sq_hi[:, j % 4, :], sq[:, j % 2, :]).then_inc(sq_hi_ready, 1)
                dve.wait_ge(sq_hi_ready, HB * u + j + 1)
                tt(sq_lo[:, j % 4, :], sq[:, j % 2, :], sq_hi[:, j % 4, :], ALU.subtract).then_inc(sq_lo_ready, 1)

            def finish(u, par):
                dve.wait_ge(vv_done, HB * u + HB)
                for i in range(2):
                    dve.wait_ge(rc_ready, 2 * u + i + 1)
                    r_i = tile(rc, 2 * i, 2)
                    tt(r_i, out_bank[par][i][:, :], r_i, ALU.mult).then_inc(rv_ready, 1)

            def mix(u, par, last=False):
                for j in range(HB):
                    squares(u, j)
                    if j == 2 and not last:
                        x2_mix(u + 1, 1 - par)
                    if j == 5 and not last:
                        x2_low(u + 1, 1 - par)
                finish(u, par)

            x2_mix(0, 0)
            x2_low(0, 0)
            mix(0, 0)
            mix(1, 1)
            with dve.Fori(1, NU // 2 - 1) as i:
                mix(2 * i, 0)
                mix(2 * i + 1, 1)
            mix(NU - 2, 0)
            mix(NU - 1, 1, last=True)

        @block.gpsimd
        def _(pool):
            tt, ts_ = nc.gpsimd.tensor_tensor, nc.gpsimd.tensor_scalar

            def tile(buf, t):
                return buf[:, t * C:(t + 1) * C]

            def norms(u):
                pool.wait_ge(ve1_ready, u + 1)
                tt(r1[:, :], ve1[:, :], half_neg[:, :], ALU.pow).then_inc(r1_ready, 1)
                pool.wait_ge(ve2_ready, u + 1)
                tt(r2[:, :], ve2[:, :], half_neg[:, :], ALU.pow).then_inc(r2_ready, 1)
                stand_alone(pool, (nb2_ready, 3 * u + 3), (xnT_done, 2 * u))
                for t in range(TU):
                    last = ts_(tile(xn, t), tile(xb, t), r1[:, t:t + 1], nb1[:, t:t + 1], ALU.mult, ALU.add)
                last.then_inc(xn_ready, 1)
                stand_alone(pool, (h2T_done, 2 * (u - 1)), (xx_lo_ready, u), (xx_hi_ready, u))
                for t in range(TU):
                    last = ts_(tile(nrm, t), tile(xb, t), s2[:, t:t + 1], nb2[:, t:t + 1], ALU.mult, ALU.add)
                last.then_inc(nrm_ready, 1)

            def copy_xn(u):
                pool.wait_ge(xn_ready, u + 1)
                nc.gpsimd.tensor_copy(z[:, u, :], xn[:, :]).then_inc(z_copied, 1)

            def scale_h(u):
                for k in range(KC):
                    stand_alone(pool, (h_ready, 2 * u + k + 1), (hT_done, 2 * u + 2))
                    ts_(xxx[:, k, :], h[:, k, 1:U + 1], tsd[:, 0, k:k + 1], 0.0,
                        ALU.mult, ALU.add).then_inc(a_ready, 1)

            def make_g(u):
                pool.wait_ge(m_ready, 4 * u + 2)
                tt(kg[:, :, :], kg[:, :, :], mm[:, :, 0:U], ALU.subtract).then_inc(g_ready, 1)

            def ln2_rstd(u):
                pool.wait_ge(ve3_ready, u + 1)
                tt(r3[:, :], ve3[:, :], half_neg[:, :], ALU.pow).then_inc(r3_ready, 1)

            def add_acc(u, par):
                pool.wait_ge(nrm2_ready, 4 * u + 4)
                pool.wait_ge(moe_added, 32 * (u + 1))
                tt(z[:, u, :], z[:, u, :], acc[:, par, :], ALU.add).then_inc(z_ready, 1)

            def finish_wkv(u, par):
                pool.wait_ge(aa_ready, 2 * u + 2)
                tt(ep[:, 0], vv[:, :, :], aa[:, :, 0:U], ALU.subtract).then_inc(v_used, 1)
                pool.wait_ge(v_used, u + 1)
                pool.wait_ge(sg_ready, 2 * u + 2)
                tt(ep[:, 0], ep[:, 0], ep[:, 1], ALU.mult).then_inc(y_own, 1)
                pool.wait_ge(y_own, 2 * u + 1)
                tt(ep[:, 0], ep[:, 0], aa[:, :, 0:U], ALU.add).then_inc(y_own, 1)
                pool.wait_ge(y_own, 2 * u + 2)
                tt(ep[:, 0], ep[:, 0], rr[:, par], ALU.mult).then_inc(y_ready, 1)

            def step(u, par, first=False, last=False):
                make_g(u)
                if not first:
                    ln2_rstd(u - 1)
                if not last:
                    norms(u + 1)
                if not first:
                    add_acc(u - 1, 1 - par)
                if not last:
                    copy_xn(u + 1)
                    scale_h(u + 1)
                finish_wkv(u, par)

            pool.wait_ge(consts_ready, 1)
            norms(0)
            copy_xn(0)
            pool.wait_ge(ts_ready, 3)
            scale_h(0)
            step(0, 0, first=True)
            pool.wait_ge(lo_split, SPLIT[4])
            with pool.Fori(0, (NU - 2) // 2) as i:
                step(2 * i + 1, 1)
                step(2 * i + 2, 0)
            step(NU - 1, 1, last=True)
            ln2_rstd(NU - 1)
            add_acc(NU - 1, 1)

            with pool.Fori(0, NU) as u:
                for i in range(2):
                    pool.wait_ge(rv_ready, 2 * u + i + 1)
                    zi = z[:, u, 2 * i * C:2 * (i + 1) * C]
                    tt(zi, zi, rc[:, 2 * i * C:2 * (i + 1) * C], ALU.add).then_inc(out_ready, 1)


_OUT = ("out", (B, T, C))


def kernel(**inputs):
    import numpy as np
    import concourse.bacc as bacc
    from concourse import mybir as mb
    from concourse.bass_utils import run_bass_kernel_spmd

    a = {k.removeprefix("L0_"): np.asarray(val) for k, val in inputs.items()}

    def rows(w):
        n = w.shape[0] // P
        return w.reshape(n, P, w.shape[1]).transpose(1, 0, 2).reshape(P, -1)

    def column(vec):
        return vec.reshape(KC, P).T

    kvr = np.concatenate([a["attn_Wk"].T, a["attn_Wv"].T, a["attn_Wr"].T], axis=1)
    we = a["ffn_We"].transpose(1, 0, 2).reshape(C, E * C)
    weights = np.concatenate([rows(w) for w in (
        kvr, a["ffn_Wg"], we, a["attn_Wck"].T, a["attn_Wcr"].T, a["attn_Wcv"].T)], axis=1)

    vectors = np.concatenate(
        [column(a["attn_" + n]) for n in ("ln1_w", "ln1_b", "ln2_w", "ln2_b")]
        + [column(a["attn_time_shift"]), column(a["attn_time_first"]),
           np.broadcast_to(np.tile(a["ffn_bg"], TU), (P, TU * E)),
           np.broadcast_to(np.tile(np.arange(E, dtype=np.float32), TU), (P, TU * E)),
           np.eye(P, dtype=np.float32)], axis=1)
    arrays = {"x": a["attn_x"], "weights": weights, "vectors": vectors, "be": a["ffn_be"]}
    arrays = {k: np.ascontiguousarray(val) for k, val in arrays.items()}

    nc = bacc.Bacc("TRN2", target_bir_lowering=False, num_devices=1, dynamic_dma_scratch_size=256)
    aps = [nc.dram_tensor(k, val.shape, mb.dt.float32, kind="ExternalInput").ap() for k, val in arrays.items()]
    aps.append(nc.dram_tensor(_OUT[0], _OUT[1], mb.dt.float32, kind="ExternalOutput").ap())
    rwkv_moe(nc, *aps)
    return run_bass_kernel_spmd(nc, [arrays], core_ids=[0]).results[0][_OUT[0]]
```

```python
import concourse.bass as bass
from concourse import mybir
from contextlib import ExitStack

P = 128
B = 4
T = 1024
C = 256
KC = C // P
U = 512
TU = U // P
NU = B * T // U
E = 8
HID = 4 * C
HB = HID // P
Q = E // 2
EPS = 1e-5

KVR0 = 0
WG0 = KVR0 + KC * 3 * C
WE0 = WG0 + KC * E
WCK0 = WE0 + KC * E * C
WCR0 = WCK0 + KC * HID
WCV0 = WCR0 + KC * C
WCOLS = WCV0 + HB * C
V_LN1W, V_LN1B, V_LN2W, V_LN2B, V_TS, V_U = (KC * i for i in range(6))
V_BG = 6 * KC
V_IOTA = V_BG + TU * E
V_ID = V_IOTA + TU * E
VCOLS = V_ID + P


def rwkv_moe(nc, x, weights, vectors, be, out):
    f32, f32r, u32 = mybir.dt.float32, mybir.dt.float32r, mybir.dt.uint32
    ALU, ACT = mybir.AluOpType, mybir.ActivationFunctionType
    x_u = x.rearrange("b (h t p) c -> (b h) p t c", h=T // U, p=P)
    out_u = out.rearrange("b (h t p) c -> (b h) p t c", h=T // U, p=P)

    with ExitStack() as ctx:
        def sb(name, shape, dt=f32):
            return ctx.enter_context(nc.sbuf_tensor(name, shape, dt))

        def sem(name):
            return ctx.enter_context(nc.semaphore(name))

        w_hi, w_lo = sb("w_hi", [P, WCV0], f32r), sb("w_lo", [P, WCV0], f32r)
        wcv_hi, wcv_lo = sb("wcv_hi", [P, WCOLS - WCV0], f32r), sb("wcv_lo", [P, WCOLS - WCV0], f32r)
        keep = sb("keep", [P, 2 * NU * TU * C])
        h2 = keep[:, 0:KC * NU * U].rearrange("p (k n) -> p k n", k=KC)
        z = keep[:, KC * NU * U:].rearrange("p (u n) -> p u n", u=NU)
        raw_a = keep[:, 0:KC * NU * U]
        RAW_A = KC * NU * U
        raw_b = keep[:, 2 * RAW_A - (WCOLS - RAW_A):2 * RAW_A]
        vec = sb("vec", [P, VCOLS])
        be_sb = sb("be_sb", [E, C])
        tsd = sb("tsd", [P, 3, KC])
        zero1 = sb("zero1", [P, 1])

        def v(col, kc=0):
            return vec[:, col + kc:col + kc + 1]
        ident = vec[:, V_ID:V_ID + P]
        iota = vec[:, V_IOTA:V_IOTA + TU * E].rearrange("p (t e) -> p t e", t=TU)
        bg = vec[:, V_BG:V_BG + TU * E].rearrange("p (t e) -> p t e", t=TU)

        xb = sb("xb", [P, TU * C])
        xn = sb("xn", [P, TU * C])
        nrm = sb("nrm", [P, TU * C])
        nrm2 = sb("nrm2", [P, TU * C])
        xnT_hi, xnT_lo = sb("xnT_hi", [P, KC, U], f32r), sb("xnT_lo", [P, KC, U], f32r)
        h = sb("h", [P, KC, U + 1])
        xx_hi, xx_lo = sb("xx_hi", [P, KC, U], f32r), sb("xx_lo", [P, KC, U], f32r)
        acc = sb("acc", [P, 2, TU * C])
        kg = sb("kg", [P, KC, U])
        vv = sb("vv", [P, KC, U])
        rr = sb("rr", [P, KC, U])
        ep = sb("ep", [P, 2, KC, U])
        sl = sb("sl", [P, KC, U + 1])
        mm = sb("mm", [P, KC, U + 1])
        aa = sb("aa", [P, KC, U + 1])
        s_last = sb("s_last", [P, KC])
        st1, st2 = sb("st1", [P, TU, 6]), sb("st2", [P, TU, 6])
        mv1, mv2 = sb("mv1", [P, TU, 2]), sb("mv2", [P, TU, 2])
        ve1, r1, nb1 = (sb(n, [P, 2, TU]) for n in ("ve1", "r1", "nb1"))
        half_neg = sb("half_neg", [P, 2, TU])
        ve3, r3, nb3 = (sb(n, [P, TU]) for n in ("ve3", "r3", "nb3"))
        lg, top = sb("lg", [P, TU, E]), sb("top", [P, TU, E])
        idx = sb("idx", [P, TU, E], u32)
        idxf = sb("idxf", [P, TU, 2])
        dif = sb("dif", [P, TU])
        tw = sb("tw", [P, 2, TU])
        hot = (lg, top)
        gate = sb("gate", [P, TU, E])
        gT = mm[0:E, 0, 0:U]

        bank = [ctx.enter_context(nc.psum_tensor(f"bank{i}", [P, U], f32)) for i in range(8)]
        XN_F, R_F, HT_F, YT_F, BIAS_F, H2_F, KV_F = (0, 1), (2, 5), (3, 4), (6, 7), (8, 9), (10, 11), range(12, 16)
        ring = [bank[f % 4] for f in range(16)]
        moe_bank = bank[4:7]
        logit_bank = gT_bank = bank[7]
        kc_bank, rc_bank = bank[4:6], bank[2:4]
        out_bank = [bank[6:8], bank[0:2]]

        vec_loaded, be_loaded = sem("vec_loaded"), sem("be_loaded")
        w_loaded = [sem(f"w_loaded{i}") for i in range(5)]
        hi_split, lo_split = sem("hi_split"), sem("lo_split")
        ts_ready, consts_ready = sem("ts_ready"), sem("consts_ready")
        x_loaded = sem("x_loaded")
        hT_done, xnT_done = sem("hT_done"), sem("xnT_done")
        kv_done, r_done = sem("kv_done"), sem("r_done")
        logits_done, gT_done = sem("logits_done"), sem("gT_done")
        bias_done = sem("bias_done")
        yT_done, h2T_done = sem("yT_done"), sem("h2T_done")
        moe_done = sem("moe_done")
        xnT_hi_ready, h_ready = sem("xnT_hi_ready"), sem("h_ready")
        kv_read, r_read = sem("kv_read"), sem("r_read")
        tw_ready, gT_ready = sem("tw_ready"), sem("gT_ready")
        eg_ready, ln_ready, ed_ready, sg_ready = (sem(n) for n in (
            "eg_ready", "ln_ready", "ed_ready", "sg_ready"))
        xx_hi_ready = sem("xx_hi_ready")
        h2_ready = sem("h2_ready")
        nrm2_ready, z_copied, x_kept = sem("nrm2_ready"), sem("z_copied"), sem("x_kept")
        xnT_lo_ready = sem("xnT_lo_ready")
        logits_read, dif_ready, gates_own, gates_ready = (sem(n) for n in (
            "logits_read", "dif_ready", "gates_own", "gates_ready"))
        acc_init = sem("acc_init")
        moe_added = sem("moe_added")
        x1_ready = sem("x1_ready")
        ln2_own, ve3_ready, nb3_ready = sem("ln2_own"), sem("ve3_ready"), sem("nb3_ready")
        m_ready, ep_clipped, s_ready, d_ready, aa_ready = (sem(n) for n in (
            "m_ready", "ep_clipped", "s_ready", "d_ready", "aa_ready"))
        wkv_own = sem("wkv_own")
        ln1_own, ve1_ready, nb1_ready = sem("ln1_own"), sem("ve1_ready"), sem("nb1_ready")
        h_first = sem("h_first")
        xxx_ready, xx_lo_ready = sem("xxx_ready"), sem("xx_lo_ready")
        g_ready, r1_ready, r3_ready = sem("g_ready"), sem("r1_ready"), sem("r3_ready")
        xn_ready, nrm_ready, z_ready = sem("xn_ready"), sem("nrm_ready"), sem("z_ready")
        a_ready = sem("a_ready")
        ep_own, ts_own = sem("ep_own"), sem("ts_own")
        v_used, y_own, y_ready = sem("v_used"), sem("y_own"), sem("y_ready")
        x2_own = sem("x2_own")
        x2_hi_ready, x2_lo_ready = sem("x2_hi_ready"), sem("x2_lo_ready")
        kc_done, relu_ready, sq_ready, sq_hi_ready, sq_lo_ready, vv_done = (sem(n) for n in (
            "kc_done", "relu_ready", "sq_ready", "sq_hi_ready", "sq_lo_ready", "vv_done"))
        rc_done, rc_ready, rv_ready, out_ready, stored, out_read = (sem(n) for n in (
            "rc_done", "rc_ready", "rv_ready", "out_ready", "stored", "out_read"))

        CHUNKS = [(0, WE0), (WE0, WE0 + 2048), (WE0 + 2048, WCK0), (WCK0, RAW_A), (RAW_A, WCOLS)]

        def raw(a, b):
            return raw_a[:, a:b] if b <= RAW_A else raw_b[:, a - RAW_A:b - RAW_A]

        def parts(a, b):
            found = []
            if a < WCV0:
                e = min(b, WCV0)
                found.append((w_hi[:, a:e], w_lo[:, a:e], raw(a, e)))
            if b > WCV0:
                s = max(a, WCV0)
                found.append((wcv_hi[:, s - WCV0:b - WCV0], wcv_lo[:, s - WCV0:b - WCV0], raw(s, b)))
            return found
        N_SPLIT = [len(parts(a, b)) for a, b in CHUNKS]
        SPLIT = [sum(N_SPLIT[:i + 1]) for i in range(len(CHUNKS))]

        def from_zero(eng, semaphore, value):
            if not isinstance(value, int) or value > 0:
                eng.wait_ge(semaphore, value)

        def stand_alone(eng, *waits):
            values = [n if isinstance(n, int) else eng.to_reg(n) for _, n in waits]
            eng.wait_ge(vec_loaded, 16)
            for (semaphore, _), n in zip(waits, values):
                from_zero(eng, semaphore, n)

        block = ctx.enter_context(nc.Block())

        sq_hi = w_hi[:, WE0:WE0 + 4 * U].rearrange("p (s n) -> p s n", s=4)
        sq_lo = w_lo[:, WE0:WE0 + 4 * U].rearrange("p (s n) -> p s n", s=4)
        relu = acc[:, 0, :].rearrange("p (s n) -> p s n", s=2)
        sq = acc[:, 1, :].rearrange("p (s n) -> p s n", s=2)
        rc = xn
        xxx = nrm[:, :].rearrange("p (k n) -> p k n", k=KC)

        @block.sync
        def _(sp):
            sp.dma_start(xb[:, :].rearrange("p (t c) -> p t c", t=TU), x_u[0]).then_inc(x_loaded, 16)
            sp.dma_start(vec[:, :], vectors).then_inc(vec_loaded, 16)
            for i, (a, b) in enumerate(CHUNKS):
                sp.dma_start(raw(a, b), weights[:, a:b]).then_inc(w_loaded[i], 16)
                if i == 0:
                    sp.dma_start(be_sb[:, :], be).then_inc(be_loaded, 16)

            def load_x(u):
                sp.wait_ge(x_kept, u)
                sp.wait_ge(xn_ready, u)
                sp.wait_ge(nrm_ready, u)
                sp.dma_start(xb[:, :].rearrange("p (t c) -> p t c", t=TU), x_u[u]).then_inc(x_loaded, 16)
            with sp.Fori(1, NU) as u:
                load_x(u)

            with sp.Fori(0, NU) as u:
                sp.wait_ge(out_ready, 2 * u + 2)
                sp.dma_start(out_u[u], z[:, u, :].rearrange("p (t c) -> p t c", t=TU)).then_inc(stored, 16)
            sp.wait_ge(stored, 16 * NU)

        @block.tensor
        def _(pe):
            mul = nc.tensor.matmul

            def wh(col, n=P):
                return w_hi[:, col:col + n]

            def wl(col, n=P):
                return w_lo[:, col:col + n]

            def h_transposes(u):
                pe.wait_ge(nrm_ready, u + 1)
                for k in range(KC):
                    if k == 0:
                        from_zero(pe, kv_read, 4 * u)
                    else:
                        from_zero(pe, xnT_lo_ready, 2 * (u - 1) + 1)
                    for t in range(TU):
                        last = nc.tensor.transpose(ring[HT_F[k]][:, t * P:(t + 1) * P],
                                                   nrm[:, t * C + k * P:t * C + (k + 1) * P], ident)
                    last.then_inc(hT_done, 1)

            def xn_transposes(u):
                pe.wait_ge(xn_ready, u + 1)
                for k in range(KC):
                    pe.wait_ge(kv_read, 4 * u + k + 1)
                    for t in range(TU):
                        last = nc.tensor.transpose(ring[XN_F[k]][:, t * P:(t + 1) * P],
                                                   xn[:, t * C + k * P:t * C + (k + 1) * P], ident)
                    last.then_inc(xnT_done, 1)

            def project(u, ps, i):
                for k in range(KC):
                    col = KVR0 + k * 3 * C + i * P
                    mul(ps[:, :], wh(col), xx_hi[:, k, :], start=(k == 0), stop=False)
                    mul(ps[:, :], wh(col), xx_lo[:, k, :], start=False, stop=False)
                    last = mul(ps[:, :], wl(col), xx_hi[:, k, :], start=False, stop=(k == KC - 1))
                return last

            def project_kv(u, i):
                if i == 0:
                    pe.wait_ge(xx_lo_ready, u + 1)
                    pe.wait_ge(xx_hi_ready, u + 1)
                if isinstance(u, int) and u <= 1:
                    pe.wait_ge(h_ready, 2)
                    from_zero(pe, r_read, 2 * u)
                if i < 2:
                    from_zero(pe, acc_init, 2 * (u - 1) + i + 1)
                else:
                    from_zero(pe, h2_ready, 2 * (u - 2) + i - 1)
                project(u, ring[KV_F[i]], i).then_inc(kv_done, 1)

            def project_r(u, i):
                if i == 0:
                    pe.wait_ge(kv_read, 4 * u + 3)
                else:
                    pe.wait_ge(xnT_lo_ready, 2 * u + 2)
                project(u, ring[R_F[i]], 4 + i).then_inc(r_done, 1)

            def logits(u):
                pe.wait_ge(xnT_lo_ready, 2 * u + 2)
                pe.wait_ge(xnT_hi_ready, 2 * u + 2)
                from_zero(pe, gT_ready, u)
                for t in range(TU):
                    ps = logit_bank[:, t * E:(t + 1) * E]
                    ts = slice(t * P, (t + 1) * P)
                    for k in range(KC):
                        col = WG0 + k * E
                        mul(ps, xnT_hi[:, k, ts], wh(col, E), start=(k == 0), stop=False)
                        mul(ps, xnT_hi[:, k, ts], wl(col, E), start=False, stop=False)
                        last = mul(ps, xnT_lo[:, k, ts], wh(col, E), start=False, stop=(k == KC - 1))
                last.then_inc(logits_done, 1)

            def y_transposes(u):
                pe.wait_ge(y_ready, u + 1)
                for i in range(2):
                    if isinstance(u, int) and u == NU - 1:
                        pe.wait_ge(h2_ready, 2 * u)
                    elif i == 0:
                        pe.wait_ge(r_read, 2 * (u + 1) + 1)
                    elif not (isinstance(u, int) and u == NU - 2):
                        pe.wait_ge(h_ready, 2 * (u + 2) + 1)
                    else:
                        pe.wait_ge(kv_read, 4 * NU)
                    for t in (2 * i, 2 * i + 1):
                        for k in range(KC):
                            at = (t % 2) * C + k * P
                            last = nc.tensor.transpose(ring[YT_F[i]][:, at:at + P],
                                                       ep[:, 0, k, t * P:(t + 1) * P], ident)
                    last.then_inc(yT_done, 1)

            def h2_transposes(u):
                pe.wait_ge(nrm2_ready, u + 1)
                for k in range(KC):
                    pe.wait_ge(x1_ready, 2 * u + k + 1)
                    for t in range(TU):
                        last = nc.tensor.transpose(ring[H2_F[k]][:, t * P:(t + 1) * P],
                                                   nrm2[:, t * C + k * P:t * C + (k + 1) * P], ident)
                    last.then_inc(h2T_done, 1)

            def gate_bias(u, last=False):
                pe.wait_ge(gates_ready, u + 1)
                for t in range(TU):
                    mm_last = nc.tensor.transpose(gT_bank[0:E, t * P:(t + 1) * P], gate[:, t, :], ident)
                mm_last.then_inc(gT_done, 1)
                pe.wait_ge(gT_ready, u + 1)
                for i in range(2):
                    if i == 1:
                        pe.wait_ge(r_read, 2 * u + 2)
                    elif not last:
                        pe.wait_ge(h_ready, 2 * (u + 1) + 2)
                    for t in (2 * i, 2 * i + 1):
                        mm_last = mul(ring[BIAS_F[i]][:, (t % 2) * C:(t % 2 + 1) * C],
                                   gT[:, t * P:(t + 1) * P], be_sb[:, :], start=True, stop=True)
                    mm_last.then_inc(bias_done, 1)

            def experts(u, f):
                t, q = f // Q, f % Q
                from_zero(pe, moe_added, 32 * u + max(2 * (f - 2), 0))
                ps = moe_bank[f % 3]
                ts = slice(t * P, (t + 1) * P)
                for k in range(KC):
                    col = WE0 + k * E * C + q * 2 * C
                    mul(ps[:, :], xnT_hi[:, k, ts], wh(col, 2 * C), start=(k == 0), stop=False)
                    mul(ps[:, :], xnT_hi[:, k, ts], wl(col, 2 * C), start=False, stop=False)
                    last = mul(ps[:, :], xnT_lo[:, k, ts], wh(col, 2 * C), start=False, stop=(k == KC - 1))
                last.then_inc(moe_done, 1)

            def step(u, first=False, last=False):
                xn_transposes(u)
                project_r(u, 0)
                if not last:
                    h_transposes(u + 1)
                logits(u)
                project_r(u, 1)
                if not first:
                    y_transposes(u - 1)
                gate_bias(u, last)
                if first:
                    pe.wait_ge(hi_split, SPLIT[2])
                    pe.wait_ge(lo_split, SPLIT[2])
                for f in range(TU * Q):
                    if f in (9, 11, 13, 15) and not last:
                        project_kv(u + 1, (f - 9) // 2)
                    experts(u, f)
                    if f == 4 and not first:
                        h2_transposes(u - 1)

            pe.wait_ge(vec_loaded, 16)
            pe.wait_ge(be_loaded, 16)
            h_transposes(0)
            pe.wait_ge(hi_split, SPLIT[0])
            pe.wait_ge(lo_split, SPLIT[0])
            for i in range(4):
                project_kv(0, i)
            step(0, first=True)
            with pe.Fori(1, NU - 1) as u:
                step(u)
            step(NU - 1, last=True)
            y_transposes(NU - 1)
            h2_transposes(NU - 1)

            x2_hi, x2_lo = (xx_hi, xnT_hi), (xx_lo, xnT_lo)

            def hidden(u, par, j):
                if j == 0:
                    pe.wait_ge(x2_lo_ready, u + 1)
                    pe.wait_ge(x2_hi_ready, u + 1)
                from_zero(pe, relu_ready, HB * u + j - 1)
                ps = kc_bank[j % 2]
                for k in range(KC):
                    col = WCK0 + k * HID + j * P
                    mul(ps[:, :], wh(col), x2_hi[par][:, k, :], start=(k == 0), stop=False)
                    mul(ps[:, :], wh(col), x2_lo[par][:, k, :], start=False, stop=False)
                    last = mul(ps[:, :], wl(col), x2_hi[par][:, k, :], start=False, stop=(k == KC - 1))
                last.then_inc(kc_done, 1)

            def receptance(u, par, i):
                from_zero(pe, rc_ready, 2 * u + i - 1)
                for t in (2 * i, 2 * i + 1):
                    ps = rc_bank[i][:, (t % 2) * C:(t % 2 + 1) * C]
                    ts = slice(t * P, (t + 1) * P)
                    for k in range(KC):
                        col = WCR0 + k * C
                        mul(ps, x2_hi[par][:, k, ts], wh(col, C), start=(k == 0), stop=False)
                        mul(ps, x2_hi[par][:, k, ts], wl(col, C), start=False, stop=False)
                        last = mul(ps, x2_lo[par][:, k, ts], wh(col, C), start=False, stop=(k == KC - 1))
                last.then_inc(rc_done, 1)

            def values(u, par, j):
                pe.wait_ge(sq_lo_ready, HB * u + j + 1)
                pe.wait_ge(sq_hi_ready, HB * u + j + 1)
                if j == 0:
                    from_zero(pe, rv_ready, 2 * (u - 1))
                hi, lo = sq_hi[:, j % 4, :], sq_lo[:, j % 4, :]
                for t in range(TU):
                    ps = out_bank[par][t // 2][:, (t % 2) * C:(t % 2 + 1) * C]
                    ts = slice(t * P, (t + 1) * P)
                    col = slice(j * C, (j + 1) * C)
                    mul(ps, hi[:, ts], wcv_hi[:, col], start=(j == 0 and t % 2 == 0), stop=False,
                        skip_group_check=True)
                    mul(ps, hi[:, ts], wcv_lo[:, col], start=False, stop=False, skip_group_check=True)
                    last = mul(ps, lo[:, ts], wcv_hi[:, col], start=False, stop=(j == HB - 1),
                               skip_group_check=True)
                last.then_inc(vv_done, 1)

            def mix(u, par):
                for j in range(HB):
                    hidden(u, par, j)
                    if j >= 2:
                        values(u, par, j - 2)
                receptance(u, par, 0)
                values(u, par, HB - 2)
                receptance(u, par, 1)
                values(u, par, HB - 1)

            pe.wait_ge(hi_split, SPLIT[4])
            pe.wait_ge(lo_split, SPLIT[4])
            pe.wait_ge(h2_ready, 2 * NU)
            mix(0, 0)
            mix(1, 1)
            with pe.Fori(1, NU // 2) as i:
                mix(2 * i, 0)
                mix(2 * i + 1, 1)

        @block.scalar
        def _(act):
            act_fn = nc.scalar.activation

            def split_hi(i):
                act.wait_ge(w_loaded[i], 16)
                for hi, _, src in parts(*CHUNKS[i]):
                    act_fn(hi, src, ACT.Copy).then_inc(hi_split, 1)

            def h_read(u):
                act.wait_ge(h_first, u + 1)
                for k in range(KC):
                    act.wait_ge(hT_done, 2 * u + k + 1)
                    act_fn(h[:, k, 1:U + 1], ring[HT_F[k]][:, :], ACT.Identity,
                           bias=v(V_LN1B, k), scale=v(V_LN1W, k)).then_inc(h_ready, 1)

            def xx_split(u):
                act.wait_ge(xxx_ready, 2 * u + 2)
                from_zero(act, r_done, 2 * u)
                act_fn(xx_hi[:, :, :], xxx, ACT.Copy).then_inc(xx_hi_ready, 1)

            def xn_read(u):
                for k in range(KC):
                    act.wait_ge(xnT_done, 2 * u + k + 1)
                    act_fn(xnT_hi[:, k, :], ring[XN_F[k]][:, :], ACT.Copy).then_inc(xnT_hi_ready, 1)

            def kv_out(u):
                for i in range(4):
                    act.wait_ge(kv_done, 4 * u + i + 1)
                    if i == 0:
                        from_zero(act, sg_ready, 2 * u)
                    if i == 2:
                        from_zero(act, v_used, u)
                    act_fn((kg, vv)[i // 2][:, i % 2, :], ring[KV_F[i]][:, :],
                           ACT.Copy).then_inc(kv_read, 1)

            def r_out(u, i):
                act.wait_ge(r_done, 2 * u + i + 1)
                from_zero(act, y_ready, u)
                act_fn(rr[:, i, :], ring[R_F[i]][:, :], ACT.Sigmoid).then_inc(r_read, 1)

            def top_weights(u):
                act.wait_ge(dif_ready, u + 1)
                act_fn(tw[:, 0, :], dif[:, :], ACT.Sigmoid).then_inc(tw_ready, 1)
                act_fn(tw[:, 1, :], dif[:, :], ACT.Sigmoid, scale=-1.0).then_inc(tw_ready, 1)

            def gT_read(u):
                act.wait_ge(gT_done, u + 1)
                act.wait_ge(g_ready, u + 1)
                act_fn(gT, gT_bank[0:E, :], ACT.Copy).then_inc(gT_ready, 1)

            def exp_g(u):
                nc.scalar.preload_act_table_set("natural_log_exp_and_others")
                act.wait_ge(g_ready, u + 1)
                from_zero(act, yT_done, 2 * u)
                act_fn(ep[:, 0], kg[:, :, :], ACT.Exp).then_inc(eg_ready, 1)
                act_fn(ep[:, 1], kg[:, :, :], ACT.Exp, scale=-1.0).then_inc(eg_ready, 1)

            def ln_s(u):
                act.wait_ge(s_ready, u + 1)
                act_fn(sl[:, :, 1:U + 1], sl[:, :, 1:U + 1], ACT.Ln).then_inc(ln_ready, 1)

            def exp_d(u):
                act.wait_ge(d_ready, u + 1)
                act_fn(ep[:, 0], kg[:, :, :], ACT.Exp).then_inc(ed_ready, 1)
                act_fn(ep[:, 1], kg[:, :, :], ACT.Exp, scale=-1.0).then_inc(ed_ready, 1)

            def sigmoid_d(u):
                act.wait_ge(aa_ready, 2 * u + 2)
                for k in range(KC):
                    act_fn(ep[:, 1, k, :], kg[:, k, :], ACT.Sigmoid, bias=v(V_U, k)).then_inc(sg_ready, 1)

            def h2_read(u):
                for k in range(KC):
                    act.wait_ge(h2T_done, 2 * u + k + 1)
                    act_fn(h2[:, k, u * U:(u + 1) * U] if isinstance(u, int) else h2[:, k, bass.ds(u * U, U)],
                           ring[H2_F[k]][:, :], ACT.Identity,
                           bias=v(V_LN2B, k), scale=v(V_LN2W, k)).then_inc(h2_ready, 1)

            def ln2_norm(u):
                from_zero(act, h2T_done, 2 * u)
                stand_alone(act, (nb3_ready, u + 1))
                for t in range(TU):
                    last = act_fn(nrm2[:, t * C:(t + 1) * C], z[:, u, t * C:(t + 1) * C], ACT.Identity,
                                  bias=nb3[:, t:t + 1], scale=r3[:, t:t + 1])
                last.then_inc(nrm2_ready, 1)

            def copy_xn(u):
                stand_alone(act, (xn_ready, u + 1))
                act_fn(z[:, u, :], xn[:, :], ACT.Copy).then_inc(z_copied, 1)

            def keep_x(u, par):
                act.wait_ge(x_loaded, 16 * (u + 1))
                from_zero(act, z_ready, u - 1)
                act_fn(acc[:, par, :], xb[:, :], ACT.Copy).then_inc(x_kept, 1)

            def step(u, par, first=False, last=False):
                xn_read(u)
                r_out(u, 0)
                if not last:
                    h_read(u + 1)
                top_weights(u)
                r_out(u, 1)
                gT_read(u)
                if first:
                    split_hi(1)
                    split_hi(2)
                exp_g(u)
                if not last:
                    xx_split(u + 1)
                if first:
                    split_hi(3)
                    split_hi(4)
                if not first:
                    ln2_norm(u - 1)
                ln_s(u)
                if not last:
                    copy_xn(u + 1)
                if not first:
                    h2_read(u - 1)
                exp_d(u)
                if not last:
                    keep_x(u + 1, 1 - par)
                sigmoid_d(u)
                if not last:
                    kv_out(u + 1)

            act.wait_ge(vec_loaded, 16)
            keep_x(0, 0)
            split_hi(0)
            h_read(0)
            xx_split(0)
            copy_xn(0)
            kv_out(0)
            step(0, 0, first=True)
            act.wait_ge(lo_split, SPLIT[4])
            with act.Fori(0, (NU - 2) // 2) as i:
                step(2 * i + 1, 1)
                step(2 * i + 2, 0)
            step(NU - 1, 1, last=True)
            ln2_norm(NU - 1)
            h2_read(NU - 1)

            x2_hi = (xx_hi, xnT_hi)

            def x2_split(u, par):
                act.wait_ge(x2_own, 3 * KC * (u + 1))
                from_zero(act, kc_done, HB * (u - 1))
                from_zero(act, rc_done, 2 * (u - 1))
                act_fn(x2_hi[par][:, :, :], xxx, ACT.Copy).then_inc(x2_hi_ready, 1)

            def mix(u, par, last=False):
                for j in range(HB):
                    act.wait_ge(kc_done, HB * u + j + 1)
                    from_zero(act, sq_ready, HB * u + j - 1)
                    act_fn(relu[:, j % 2, :], kc_bank[j % 2][:, :], ACT.Relu).then_inc(relu_ready, 1)
                    act.wait_ge(relu_ready, HB * u + j + 1)
                    from_zero(act, sq_lo_ready, HB * u + j - 1)
                    from_zero(act, sq_hi_ready, HB * u + j - 1)
                    act_fn(sq[:, j % 2, :], relu[:, j % 2, :], ACT.Square).then_inc(sq_ready, 1)
                    if j == 4 and not last:
                        x2_split(u + 1, 1 - par)
                for i in range(2):
                    act.wait_ge(rc_done, 2 * u + i + 1)
                    from_zero(act, out_ready, 2 * u + i - 1)
                    act_fn(rc[:, i * 2 * C:(i + 1) * 2 * C], rc_bank[i][:, :],
                           ACT.Sigmoid).then_inc(rc_ready, 1)

            x2_split(0, 0)
            act.wait_ge(z_ready, NU)
            mix(0, 0)
            mix(1, 1)
            with act.Fori(1, NU // 2 - 1) as i:
                mix(2 * i, 0)
                mix(2 * i + 1, 1)
            mix(NU - 2, 0)
            mix(NU - 1, 1, last=True)

        @block.vector
        def _(dve):
            tt, ts_, stt = nc.vector.tensor_tensor, nc.vector.tensor_scalar, nc.vector.scalar_tensor_tensor
            scan = nc.vector.tensor_tensor_scan
            copy = nc.vector.tensor_copy

            def tile(buf, t, n=1):
                return buf[:, t * C:(t + n) * C]

            def split_lo(i):
                dve.wait_ge(hi_split, SPLIT[i])
                for hi, lo, src in parts(*CHUNKS[i]):
                    tt(lo, src, hi, ALU.subtract).then_inc(lo_split, 1)

            def ln1_stats(u):
                dve.wait_ge(x_loaded, 16 * (u + 1))
                for t in range(TU):
                    nc.vector.bn_stats(st1[:, t, :], tile(xb, t)).then_inc(ln1_own, 1)

            def ln1_variances(u):
                stand_alone(dve, (ln1_own, 8 * u + 4))
                for t in range(TU):
                    nc.vector.bn_aggr(mv1[:, t, :], st1[:, t, :]).then_inc(ln1_own, 1)
                dve.wait_ge(ln1_own, 8 * u + 8)
                ts_(ve1[:, 0, :], mv1[:, :, 1], EPS, None, ALU.add).then_inc(ve1_ready, 1)
                ts_(ve1[:, 1, :], mv1[:, :, 1], 1.0 + EPS, EPS * EPS, ALU.mult, ALU.add).then_inc(ve1_ready, 1)

            def ln1_coefficients(u):
                dve.wait_ge(r1_ready, u + 1)
                for n in range(2):
                    stt(nb1[:, n, :], mv1[:, :, 0], -1.0, r1[:, n, :], ALU.mult, ALU.mult).then_inc(nb1_ready, 1)

            def h_column(start):
                if start:
                    copy(h[:, :, 0], vec[:, V_TS:V_TS + KC]).then_inc(h_first, 1)
                else:
                    copy(h[:, :, 0], h[:, :, U]).then_inc(h_first, 1)

            def xxx_mix(u, next_starts, last=False):
                for k in range(KC):
                    dve.wait_ge(a_ready, 2 * u + k + 1)
                    stt(xxx[:, k, :], h[:, k, 0:U], tsd[:, 1, k:k + 1], xxx[:, k, :],
                        ALU.mult, ALU.add).then_inc(xxx_ready, 1)
                if not last:
                    dve.wait_ge(xxx_ready, 2 * u + 2)
                    h_column(next_starts)

            def xx_low(u):
                dve.wait_ge(xx_hi_ready, u + 1)
                tt(xx_lo[:, :, :], xxx, xx_hi[:, :, :], ALU.subtract).then_inc(xx_lo_ready, 1)

            def xn_low(u):
                for k in range(KC):
                    dve.wait_ge(xnT_hi_ready, 2 * u + k + 1)
                    tt(xnT_lo[:, k, :], ring[XN_F[k]][:, :], xnT_hi[:, k, :],
                       ALU.subtract).then_inc(xnT_lo_ready, 1)

            def gates(u):
                dve.wait_ge(logits_done, u + 1)
                tt(lg[:, :, :], logit_bank[:, 0:TU * E].rearrange("p (t e) -> p t e", t=TU), bg,
                   ALU.add).then_inc(logits_read, 1)
                stand_alone(dve, (logits_read, u + 1))
                for t in range(TU):
                    nc.vector.max(top[:, t, :], lg[:, t, :]).then_inc(gates_own, 1)
                dve.wait_ge(gates_own, 13 * u + 4)
                tt(dif[:, :], top[:, :, 0], top[:, :, 1], ALU.subtract).then_inc(dif_ready, 1)
                for t in range(TU):
                    nc.vector.max_index(idx[:, t, :], top[:, t, :], lg[:, t, :]).then_inc(gates_own, 1)
                dve.wait_ge(gates_own, 13 * u + 8)
                copy(idxf[:, :, :], idx[:, :, 0:2]).then_inc(gates_own, 1)
                dve.wait_ge(gates_own, 13 * u + 9)
                for n in range(2):
                    tt(hot[n][:, :, :], iota, idxf[:, :, n:n + 1].to_broadcast([P, TU, E]),
                       ALU.is_equal).then_inc(gates_own, 1)
                dve.wait_ge(gates_own, 13 * u + 11)
                dve.wait_ge(tw_ready, 2 * u + 2)
                for n in range(2):
                    tt(hot[n][:, :, :], hot[n][:, :, :], tw[:, n, :].unsqueeze(2).to_broadcast([P, TU, E]),
                       ALU.mult).then_inc(gates_own, 1)
                dve.wait_ge(gates_own, 13 * u + 13)
                tt(gate[:, :, :], hot[0][:, :, :], hot[1][:, :, :], ALU.add).then_inc(gates_ready, 1)

            def start_acc(u, par):
                dve.wait_ge(x_kept, u + 1)
                for i in range(2):
                    dve.wait_ge(bias_done, 2 * u + i + 1)
                    a = tile(acc[:, par], 2 * i, 2)
                    tt(a, a, ring[BIAS_F[i]][:, :], ALU.add).then_inc(acc_init, 1)

            def add_expert(u, par, f, n):
                t, q = f // Q, f % Q
                if f == 0 and n == 0:
                    dve.wait_ge(acc_init, 2 * u + 2)
                if n == 0:
                    dve.wait_ge(moe_done, TU * Q * u + f + 1)
                dve.wait_ge(moe_added, 32 * u + 2 * f + n)
                a = tile(acc[:, par], t)
                stt(a, moe_bank[f % 3][:, n * C:(n + 1) * C], gate[:, t, 2 * q + n:2 * q + n + 1], a,
                    ALU.mult, ALU.add).then_inc(moe_added, 1)

            def add_experts(u, par, f):
                add_expert(u, par, f, 0)
                add_expert(u, par, f, 1)

            def add_y(u):
                dve.wait_ge(z_copied, u + 1)
                for i in range(2):
                    dve.wait_ge(yT_done, 2 * u + i + 1)
                    zi = z[:, u, 2 * i * C:2 * (i + 1) * C]
                    tt(zi, zi, ring[YT_F[i]][:, :], ALU.add).then_inc(x1_ready, 1)

            def ln2_stats(u):
                stand_alone(dve, (x1_ready, 2 * u + 2))
                for t in range(TU):
                    nc.vector.bn_stats(st2[:, t, :], z[:, u, t * C:(t + 1) * C]).then_inc(ln2_own, 1)
                stand_alone(dve, (ln2_own, 8 * u + 4))
                for t in range(TU):
                    nc.vector.bn_aggr(mv2[:, t, :], st2[:, t, :]).then_inc(ln2_own, 1)
                dve.wait_ge(ln2_own, 8 * u + 8)
                ts_(ve3[:, :], mv2[:, :, 1], EPS, None, ALU.add).then_inc(ve3_ready, 1)

            def ln2_coefficients(u):
                dve.wait_ge(r3_ready, u + 1)
                stt(nb3[:, :], mv2[:, :, 0], -1.0, r3[:, :], ALU.mult, ALU.mult).then_inc(nb3_ready, 1)

            def wkv_max(u, start):
                from_zero(dve, g_ready, u)
                if start:
                    nc.vector.memset(mm[:, :, 0], 0.0).then_inc(wkv_own, 1)
                else:
                    copy(mm[:, :, 0], mm[:, :, U]).then_inc(wkv_own, 1)
                dve.wait_ge(wkv_own, 4 * u + 1)
                for k in range(KC):
                    dve.wait_ge(kv_read, 4 * u + k + 1)
                    scan(mm[:, k, 1:U + 1], kg[:, k, :], zero1[:, 0:1].to_broadcast([P, U]),
                         mm[:, k, 0:1], ALU.max, ALU.max).then_inc(m_ready, 1)

            def wkv_clip(u):
                dve.wait_ge(eg_ready, 2 * u + 2)
                ts_(ep[:, :, :, :], ep[:, :, :, :], 1.0, None, ALU.min).then_inc(ep_clipped, 1)
                dve.wait_ge(ep_clipped, u + 1)

            def wkv_carry(u, start):
                if start:
                    nc.vector.memset(sl[:, :, 0], 0.0).then_inc(wkv_own, 1)
                    nc.vector.memset(s_last[:, :], 1.0).then_inc(wkv_own, 1)
                else:
                    copy(sl[:, :, 0], sl[:, :, U]).then_inc(wkv_own, 2)
            def wkv_sum(u):
                dve.wait_ge(wkv_own, 4 * u + 3)
                for k in range(KC):
                    scan(sl[:, k, 1:U + 1], ep[:, 1, k, :], ep[:, 0, k, :], s_last[:, k:k + 1],
                         ALU.mult, ALU.add).then_inc(m_ready, 1)
                dve.wait_ge(m_ready, 4 * u + 4)
                copy(s_last[:, :], sl[:, :, U]).then_inc(s_ready, 1)

            def wkv_d(u):
                dve.wait_ge(ln_ready, u + 1)
                tt(kg[:, :, :], kg[:, :, :], sl[:, :, 0:U], ALU.subtract).then_inc(d_ready, 1)

            def wkv_clip_a(u, start):
                dve.wait_ge(ed_ready, 2 * u + 2)
                ts_(ep[:, 1], ep[:, 1], 1.0, None, ALU.min).then_inc(ep_own, 1)
                from_zero(dve, y_ready, u)
                if start:
                    nc.vector.memset(aa[:, :, 0], 0.0).then_inc(wkv_own, 1)
                else:
                    copy(aa[:, :, 0], aa[:, :, U]).then_inc(wkv_own, 1)

            def wkv_cv(u):
                dve.wait_ge(kv_read, 4 * u + 4)
                stt(ep[:, 0], ep[:, 0], 1.0, vv[:, :, :], ALU.min, ALU.mult).then_inc(ep_own, 1)

            def wkv_aa(u):
                dve.wait_ge(ep_own, 2 * u + 2)
                dve.wait_ge(wkv_own, 4 * u + 4)
                for k in range(KC):
                    scan(aa[:, k, 1:U + 1], ep[:, 1, k, :], ep[:, 0, k, :], aa[:, k, 0:1],
                         ALU.mult, ALU.add).then_inc(aa_ready, 1)

            def step(u, par, start, first=False, last=False, second_last=False):
                wkv_max(u, start)
                xn_low(u)
                gates(u)
                if first:
                    split_lo(1)
                else:
                    add_y(u - 1)
                if not last:
                    xxx_mix(u + 1, next_starts=start, last=second_last)
                if not first:
                    ln2_stats(u - 1)
                if first:
                    split_lo(2)
                start_acc(u, par)
                add_expert(u, par, 0, 0)
                wkv_carry(u, start)
                wkv_clip(u)
                add_expert(u, par, 0, 1)
                if not first:
                    ln2_coefficients(u - 1)
                if not last:
                    xx_low(u + 1)
                add_expert(u, par, 1, 0)
                wkv_sum(u)
                add_expert(u, par, 1, 1)
                add_experts(u, par, 2)
                add_experts(u, par, 3)
                wkv_d(u)
                add_experts(u, par, 4)
                add_expert(u, par, 5, 0)
                wkv_clip_a(u, start)
                add_expert(u, par, 5, 1)
                wkv_cv(u)
                add_experts(u, par, 6)
                wkv_aa(u)
                for f in (7, 8, 9, 10, 11):
                    add_experts(u, par, f)
                if first:
                    split_lo(3)
                    split_lo(4)
                add_expert(u, par, 12, 0)
                if not last and not second_last:
                    ln1_stats(u + 2)
                add_expert(u, par, 12, 1)
                add_expert(u, par, 13, 0)
                if not last and not second_last:
                    ln1_variances(u + 2)
                add_expert(u, par, 13, 1)
                add_experts(u, par, 14)
                add_expert(u, par, 15, 0)
                if not last and not second_last:
                    ln1_coefficients(u + 2)
                add_expert(u, par, 15, 1)

            nc.vector.memset(zero1[:, :], 0.0).then_inc(ts_own, 1)
            nc.vector.memset(half_neg[:, :, :], -0.5).then_inc(consts_ready, 1)
            ln1_stats(0)
            ln1_variances(0)
            ts_row = vec[:, V_TS:V_TS + KC]
            ts_(tsd[:, 0, :], ts_row, 1.0, None, ALU.add).then_inc(ts_ready, 1)
            ts_(tsd[:, 1, :], ts_row, -1.0, None, ALU.mult).then_inc(ts_ready, 1)
            ts_(tsd[:, 2, :], ts_row, -1.0, 1.0, ALU.mult, ALU.add).then_inc(ts_ready, 1)
            h_column(True)
            ln1_coefficients(0)
            split_lo(0)
            dve.wait_ge(ts_ready, 3)
            dve.wait_ge(ts_own, 1)
            xxx_mix(0, next_starts=False)
            xx_low(0)
            ln1_stats(1)
            ln1_variances(1)
            ln1_coefficients(1)
            step(0, 0, True, first=True)
            with dve.Fori(0, (NU - 4) // 2) as i:
                step(2 * i + 1, 1, False)
                step(2 * i + 2, 0, True)
            step(NU - 3, 1, False)
            step(NU - 2, 0, True, second_last=True)
            step(NU - 1, 1, False, last=True)
            add_y(NU - 1)
            ln2_stats(NU - 1)
            ln2_coefficients(NU - 1)

            x2_hi, x2_lo = (xx_hi, xnT_hi), (xx_lo, xnT_lo)

            def x2_mix(u, half):
                dve.wait_ge(h2_ready, 2 * NU)
                from_zero(dve, x2_hi_ready, u)
                for k in range(KC):
                    ts_(xxx[:, k, :], h2[:, k, bass.ds(u * U, U)], tsd[:, 2, k:k + 1], None,
                        ALU.mult).then_inc(x2_own, 1)
                for k in range(KC):
                    dve.wait_ge(x2_own, 3 * KC * u + k + 1)
                    ts_k = v(V_TS, k)
                    if half == 0:
                        stt(xxx[:, k, 1:U], h2[:, k, bass.ds(u * U, U - 1)], ts_k, xxx[:, k, 1:U],
                            ALU.mult, ALU.add).then_inc(x2_own, 1)
                        stt(xxx[:, k, 0:1], h2[:, k, bass.ds(u * U + T - 1, 1)], ts_k, xxx[:, k, 0:1],
                            ALU.mult, ALU.add).then_inc(x2_own, 1)
                    else:
                        stt(xxx[:, k, :], h2[:, k, bass.ds(u * U - 1, U)], ts_k, xxx[:, k, :],
                            ALU.mult, ALU.add).then_inc(x2_own, 2)

            def x2_low(u, par):
                dve.wait_ge(x2_hi_ready, u + 1)
                tt(x2_lo[par][:, :, :], xxx, x2_hi[par][:, :, :], ALU.subtract).then_inc(x2_lo_ready, 1)

            def squares(u, j):
                dve.wait_ge(sq_ready, HB * u + j + 1)
                from_zero(dve, vv_done, HB * u + j - 3)
                copy(sq_hi[:, j % 4, :], sq[:, j % 2, :]).then_inc(sq_hi_ready, 1)
                dve.wait_ge(sq_hi_ready, HB * u + j + 1)
                tt(sq_lo[:, j % 4, :], sq[:, j % 2, :], sq_hi[:, j % 4, :], ALU.subtract).then_inc(sq_lo_ready, 1)

            def finish(u, par):
                dve.wait_ge(vv_done, HB * u + HB)
                for i in range(2):
                    dve.wait_ge(rc_ready, 2 * u + i + 1)
                    r_i = tile(rc, 2 * i, 2)
                    tt(r_i, out_bank[par][i][:, :], r_i, ALU.mult).then_inc(rv_ready, 1)

            def mix(u, par, last=False):
                for j in range(HB):
                    squares(u, j)
                    if j == 2 and not last:
                        x2_mix(u + 1, 1 - par)
                    if j == 5 and not last:
                        x2_low(u + 1, 1 - par)
                finish(u, par)

            x2_mix(0, 0)
            x2_low(0, 0)
            mix(0, 0)
            mix(1, 1)
            with dve.Fori(1, NU // 2 - 1) as i:
                mix(2 * i, 0)
                mix(2 * i + 1, 1)
            mix(NU - 2, 0)
            mix(NU - 1, 1, last=True)

        @block.gpsimd
        def _(pool):
            tt, ts_ = nc.gpsimd.tensor_tensor, nc.gpsimd.tensor_scalar

            def tile(buf, t):
                return buf[:, t * C:(t + 1) * C]

            def ln1_norm(u):
                pool.wait_ge(ve1_ready, 2 * u + 2)
                tt(r1[:, :, :], ve1[:, :, :], half_neg[:, :, :], ALU.pow).then_inc(r1_ready, 1)
                stand_alone(pool, (nb1_ready, 2 * u + 2), (xx_lo_ready, u), (xx_hi_ready, u))
                for t in range(TU):
                    last = ts_(tile(nrm, t), tile(xb, t), r1[:, 1, t:t + 1], nb1[:, 1, t:t + 1],
                               ALU.mult, ALU.add)
                last.then_inc(nrm_ready, 1)

            def make_xn(u):
                stand_alone(pool, (xnT_done, 2 * u), (z_copied, u))
                for t in range(TU):
                    last = ts_(tile(xn, t), tile(xb, t), r1[:, 0, t:t + 1], nb1[:, 0, t:t + 1],
                               ALU.mult, ALU.add)
                last.then_inc(xn_ready, 1)

            def scale_h(u):
                for k in range(KC):
                    stand_alone(pool, (h_ready, 2 * u + k + 1), (hT_done, 2 * u + 2))
                    ts_(xxx[:, k, :], h[:, k, 1:U + 1], tsd[:, 0, k:k + 1], 0.0,
                        ALU.mult, ALU.add).then_inc(a_ready, 1)

            def make_g(u):
                pool.wait_ge(m_ready, 4 * u + 2)
                tt(kg[:, :, :], kg[:, :, :], mm[:, :, 0:U], ALU.subtract).then_inc(g_ready, 1)

            def ln2_rstd(u):
                pool.wait_ge(ve3_ready, u + 1)
                from_zero(pool, nrm2_ready, u)
                tt(r3[:, :], ve3[:, :], half_neg[:, 0, :], ALU.pow).then_inc(r3_ready, 1)

            def add_acc(u, par):
                pool.wait_ge(nrm2_ready, u + 1)
                pool.wait_ge(moe_added, 32 * (u + 1))
                tt(z[:, u, :], z[:, u, :], acc[:, par, :], ALU.add).then_inc(z_ready, 1)

            def finish_wkv(u):
                pool.wait_ge(aa_ready, 2 * u + 2)
                tt(ep[:, 0], vv[:, :, :], aa[:, :, 0:U], ALU.subtract).then_inc(v_used, 1)
                pool.wait_ge(v_used, u + 1)
                pool.wait_ge(sg_ready, 2 * u + 2)
                tt(ep[:, 0], ep[:, 0], ep[:, 1], ALU.mult).then_inc(y_own, 1)
                pool.wait_ge(y_own, 2 * u + 1)
                tt(ep[:, 0], ep[:, 0], aa[:, :, 0:U], ALU.add).then_inc(y_own, 1)
                pool.wait_ge(y_own, 2 * u + 2)
                tt(ep[:, 0], ep[:, 0], rr[:, :, :], ALU.mult).then_inc(y_ready, 1)

            def step(u, par, first=False, last=False, second_last=False):
                make_g(u)
                if not last:
                    scale_h(u + 1)
                    make_xn(u + 1)
                if not first:
                    ln2_rstd(u - 1)
                    add_acc(u - 1, 1 - par)
                finish_wkv(u)
                if not last and not second_last:
                    ln1_norm(u + 2)

            pool.wait_ge(consts_ready, 1)
            ln1_norm(0)
            make_xn(0)
            pool.wait_ge(ts_ready, 3)
            scale_h(0)
            ln1_norm(1)
            step(0, 0, first=True)
            with pool.Fori(0, (NU - 4) // 2) as i:
                step(2 * i + 1, 1)
                step(2 * i + 2, 0)
            step(NU - 3, 1)
            step(NU - 2, 0, second_last=True)
            step(NU - 1, 1, last=True)
            ln2_rstd(NU - 1)
            add_acc(NU - 1, 1)

            with pool.Fori(0, NU) as u:
                for i in range(2):
                    pool.wait_ge(rv_ready, 2 * u + i + 1)
                    zi = z[:, u, 2 * i * C:2 * (i + 1) * C]
                    tt(zi, zi, rc[:, 2 * i * C:2 * (i + 1) * C], ALU.add).then_inc(out_ready, 1)


_OUT = ("out", (B, T, C))


def kernel(**inputs):
    import numpy as np
    import concourse.bacc as bacc
    from concourse import mybir as mb
    from concourse.bass_utils import run_bass_kernel_spmd

    a = {k.removeprefix("L0_"): np.asarray(val) for k, val in inputs.items()}

    def rows(w):
        n = w.shape[0] // P
        return w.reshape(n, P, w.shape[1]).transpose(1, 0, 2).reshape(P, -1)

    def column(vec):
        return vec.reshape(KC, P).T

    kvr = np.concatenate([a["attn_Wk"].T, a["attn_Wv"].T, a["attn_Wr"].T], axis=1)
    we = a["ffn_We"].transpose(1, 0, 2).reshape(C, E * C)
    weights = np.concatenate([rows(w) for w in (
        kvr, a["ffn_Wg"], we, a["attn_Wck"].T, a["attn_Wcr"].T, a["attn_Wcv"].T)], axis=1)

    vectors = np.concatenate(
        [column(a["attn_" + n]) for n in ("ln1_w", "ln1_b", "ln2_w", "ln2_b")]
        + [column(a["attn_time_shift"]), column(a["attn_time_first"]),
           np.broadcast_to(np.tile(a["ffn_bg"], TU), (P, TU * E)),
           np.broadcast_to(np.tile(np.arange(E, dtype=np.float32), TU), (P, TU * E)),
           np.eye(P, dtype=np.float32)], axis=1)
    arrays = {"x": a["attn_x"], "weights": weights, "vectors": vectors, "be": a["ffn_be"]}
    arrays = {k: np.ascontiguousarray(val) for k, val in arrays.items()}

    nc = bacc.Bacc("TRN2", target_bir_lowering=False, num_devices=1, dynamic_dma_scratch_size=256)
    aps = [nc.dram_tensor(k, val.shape, mb.dt.float32, kind="ExternalInput").ap() for k, val in arrays.items()]
    aps.append(nc.dram_tensor(_OUT[0], _OUT[1], mb.dt.float32, kind="ExternalOutput").ap())
    rwkv_moe(nc, *aps)
    return run_bass_kernel_spmd(nc, [arrays], core_ids=[0]).results[0][_OUT[0]]
```

```python
import concourse.bass as bass
from concourse import mybir
from contextlib import ExitStack

P = 128
B = 4
T = 1024
C = 256
KC = C // P
U = 512
TU = U // P
NU = B * T // U
E = 8
HID = 4 * C
HB = HID // P
Q = E // 2
EPS = 1e-5

KVR0 = 0
WG0 = KVR0 + KC * 3 * C
WE0 = WG0 + KC * E
WCK0 = WE0 + KC * E * C
WCR0 = WCK0 + KC * HID
WCV0 = WCR0 + KC * C
WCOLS = WCV0 + HB * C
V_LN1W, V_LN1B, V_LN2W, V_LN2B, V_TS, V_U = (KC * i for i in range(6))
V_BG = 6 * KC
V_BE_S, V_BE_G = V_BG + 1, V_BG + 2
V_IOTA = V_BG + 3
V_ID = V_IOTA + E
VCOLS = V_ID + P


def rwkv_moe(nc, x, weights, vectors, be, out):
    f32, f32r, u32 = mybir.dt.float32, mybir.dt.float32r, mybir.dt.uint32
    ALU, ACT = mybir.AluOpType, mybir.ActivationFunctionType
    x_u = x.rearrange("b (h t p) c -> (b h) p t c", h=T // U, p=P)
    out_u = out.rearrange("b (h t p) c -> (b h) p t c", h=T // U, p=P)

    with ExitStack() as ctx:
        def sb(name, shape, dt=f32):
            return ctx.enter_context(nc.sbuf_tensor(name, shape, dt))

        def sem(name):
            return ctx.enter_context(nc.semaphore(name))

        w_hi, w_lo = sb("w_hi", [P, WCV0], f32r), sb("w_lo", [P, WCV0], f32r)
        wcv_hi, wcv_lo = sb("wcv_hi", [P, WCOLS - WCV0], f32r), sb("wcv_lo", [P, WCOLS - WCV0], f32r)
        keep = sb("keep", [P, 2 * NU * TU * C])
        h2 = keep[:, 0:KC * NU * U].rearrange("p (k n) -> p k n", k=KC)
        z = keep[:, KC * NU * U:].rearrange("p (u n) -> p u n", u=NU)
        raw_a = keep[:, 0:KC * NU * U]
        RAW_A = KC * NU * U
        raw_b = keep[:, 2 * RAW_A - (WCOLS - RAW_A):2 * RAW_A]
        vec = sb("vec", [P, VCOLS])
        be3 = sb("be3", [3 * E, C], f32r)
        gate3 = sb("gate3", [P, TU, 3 * E])
        gate_hi = sb("gate_hi", [P, TU, E], f32r)
        gate = gate3[:, :, 0:E]
        tsd = sb("tsd", [P, 3, KC])
        zero1 = sb("zero1", [P, 1])

        def v(col, kc=0):
            return vec[:, col + kc:col + kc + 1]
        ident = vec[:, V_ID:V_ID + P]
        iota = vec[:, V_IOTA:V_IOTA + E].unsqueeze(1).to_broadcast([P, TU, E])

        xb = sb("xb", [P, TU * C])
        xn = sb("xn", [P, TU * C])
        nrm = sb("nrm", [P, TU * C])
        nrm2 = sb("nrm2", [P, TU * C])
        xnT_hi, xnT_lo = sb("xnT_hi", [P, KC, U], f32r), sb("xnT_lo", [P, KC, U], f32r)
        h = sb("h", [P, KC, U + 1])
        xx_hi, xx_lo = sb("xx_hi", [P, KC, U], f32r), sb("xx_lo", [P, KC, U], f32r)
        acc = sb("acc", [P, 2, TU * C])
        kg = sb("kg", [P, KC, U])
        vv = sb("vv", [P, KC, U])
        rr = sb("rr", [P, KC, U])
        ep = sb("ep", [P, 2, KC, U])
        sl = sb("sl", [P, KC, U + 1])
        mm = sb("mm", [P, KC, U + 1])
        aa = sb("aa", [P, KC, U + 1])
        s_last = sb("s_last", [P, KC])
        st1, st2 = sb("st1", [P, TU, 6]), sb("st2", [P, TU, 6])
        mv1, mv2 = sb("mv1", [P, TU, 2]), sb("mv2", [P, TU, 2])
        ve1, r1, nb1 = (sb(n, [P, 2, TU]) for n in ("ve1", "r1", "nb1"))
        half_neg = sb("half_neg", [P, 2, TU])
        ve3, r3, nb3 = (sb(n, [P, TU]) for n in ("ve3", "r3", "nb3"))
        lg, top = sb("lg", [P, TU, E]), sb("top", [P, TU, E])
        idx = sb("idx", [P, TU, E], u32)
        idxf = sb("idxf", [P, TU, 2])
        dif = sb("dif", [P, TU])
        ex = sb("ex", [P, TU])
        tw = sb("tw", [P, 2, TU])
        hot = (lg, top)
        lgT = sl[0:E, 0, 1:U + 1]
        gT3 = xx_lo[0:3 * E, 1, :]
        be_raw = nrm2[0:3 * E, 0:C]

        bank = [ctx.enter_context(nc.psum_tensor(f"bank{i}", [P, U], f32)) for i in range(8)]
        XN_F, R_F, YT_F, HT_F, BIAS_F, H2_F, KV_F = (0, 1), (2, 3), (4, 5), (6, 7), (8, 9), (10, 11), range(12, 16)
        ring = [bank[f % 4] for f in range(16)]
        moe_bank = bank[4:7]
        logit_bank = gT_bank = bank[7]
        kc_bank, rc_bank = (bank[5], bank[4]), bank[2:4]
        out_bank = [bank[6:8], bank[0:2]]

        vec_loaded, be_loaded = sem("vec_loaded"), sem("be_loaded")
        w_loaded = [sem(f"w_loaded{i}") for i in range(5)]
        hi_split, lo_split, lo_split_3 = sem("hi_split"), sem("lo_split"), sem("lo_split_3")
        ts_ready, consts_ready = sem("ts_ready"), sem("consts_ready")
        x_loaded = sem("x_loaded")
        hT_done, xnT_done = sem("hT_done"), sem("xnT_done")
        kv_done, r_done = sem("kv_done"), sem("r_done")
        logits_done, logits_turned, gT_done = (sem(n) for n in (
            "logits_done", "logits_turned", "gT_done"))
        bias_done = sem("bias_done")
        yT_done, h2T_done = sem("yT_done"), sem("h2T_done")
        moe_done = sem("moe_done")
        xnT_hi_ready, h_ready = sem("xnT_hi_ready"), sem("h_ready")
        kv_read, r_read = sem("kv_read"), sem("r_read")
        lgT_ready, ex_ready, gT_ready = sem("lgT_ready"), sem("ex_ready"), sem("gT_ready")
        be_hi_ready = sem("be_hi_ready")
        eg_ready, ln_ready, ed_ready, sg_ready = (sem(n) for n in (
            "eg_ready", "ln_ready", "ed_ready", "sg_ready"))
        relu_g_ready = sem("relu_g_ready")
        xx_hi_ready = sem("xx_hi_ready")
        h2_ready = sem("h2_ready")
        nrm2_ready, z_copied, x_kept = sem("nrm2_ready"), sem("z_copied"), sem("x_kept")
        xnT_lo_ready = sem("xnT_lo_ready")
        logits_read, dif_ready, gates_own, gate_hi_ready, gates_ready = (sem(n) for n in (
            "logits_read", "dif_ready", "gates_own", "gate_hi_ready", "gates_ready"))
        tw_own, be_ready = sem("tw_own"), sem("be_ready")
        acc_biased = sem("acc_biased")
        moe_added = sem("moe_added")
        x1_ready = sem("x1_ready")
        ln2_own, ve3_ready, nb3_ready = sem("ln2_own"), sem("ve3_ready"), sem("nb3_ready")
        m_ready, s_ready, aa_ready = sem("m_ready"), sem("s_ready"), sem("aa_ready")
        wkv_own, ep_own, zero_ready = sem("wkv_own"), sem("ep_own"), sem("zero_ready")
        ln1_own, ve1_ready, nb1_ready = sem("ln1_own"), sem("ve1_ready"), sem("nb1_ready")
        h_first = sem("h_first")
        xxx_ready, xx_lo_ready = sem("xxx_ready"), sem("xx_lo_ready")
        g_ready, d_ready, r1_ready, r3_ready = (sem(n) for n in ("g_ready", "d_ready", "r1_ready", "r3_ready"))
        xn_ready, nrm_ready, z_ready = sem("xn_ready"), sem("nrm_ready"), sem("z_ready")
        a_ready = sem("a_ready")
        v_used, y_own, y_ready = sem("v_used"), sem("y_own"), sem("y_ready")
        x2_own = sem("x2_own")
        x2_hi_ready, x2_lo_ready = sem("x2_hi_ready"), sem("x2_lo_ready")
        kc_done, relu_ready, sq_ready, sq_hi_ready, sq_lo_ready, vv_done = (sem(n) for n in (
            "kc_done", "relu_ready", "sq_ready", "sq_hi_ready", "sq_lo_ready", "vv_done"))
        rc_done, rc_ready, rv_ready, out_ready, stored = (sem(n) for n in (
            "rc_done", "rc_ready", "rv_ready", "out_ready", "stored"))

        CHUNKS = [(0, WE0), (WE0, WE0 + 2048), (WE0 + 2048, WCK0), (WCK0, RAW_A), (RAW_A, WCOLS)]

        def raw(a, b):
            return raw_a[:, a:b] if b <= RAW_A else raw_b[:, a - RAW_A:b - RAW_A]

        def parts(a, b):
            found = []
            if a < WCV0:
                e = min(b, WCV0)
                found.append((w_hi[:, a:e], w_lo[:, a:e], raw(a, e)))
            if b > WCV0:
                s = max(a, WCV0)
                found.append((wcv_hi[:, s - WCV0:b - WCV0], wcv_lo[:, s - WCV0:b - WCV0], raw(s, b)))
            return found
        N_SPLIT = [len(parts(a, b)) for a, b in CHUNKS]
        SPLIT = [sum(N_SPLIT[:i + 1]) for i in range(len(CHUNKS))]
        LO_SPLIT = SPLIT[4] - N_SPLIT[3]

        def added_by(f):
            return 2 * f + 3 - f % 2

        def from_zero(eng, semaphore, value):
            if not isinstance(value, int) or value > 0:
                eng.wait_ge(semaphore, value)

        def stand_alone(eng, *waits):
            values = [n if isinstance(n, int) else eng.to_reg(n) for _, n in waits]
            eng.wait_ge(vec_loaded, 16)
            for (semaphore, _), n in zip(waits, values):
                from_zero(eng, semaphore, n)

        block = ctx.enter_context(nc.Block())

        sq_hi = w_hi[:, WE0:WE0 + 4 * U].rearrange("p (s n) -> p s n", s=4)
        sq_lo = w_lo[:, WE0:WE0 + 4 * U].rearrange("p (s n) -> p s n", s=4)
        relu = acc[:, 0, :].rearrange("p (s n) -> p s n", s=2)
        sq = xb[:, :].rearrange("p (s n) -> p s n", s=2)
        rc = xn
        xxx = nrm[:, :].rearrange("p (k n) -> p k n", k=KC)

        @block.sync
        def _(sp):
            sp.dma_start(xb[:, :].rearrange("p (t c) -> p t c", t=TU), x_u[0]).then_inc(x_loaded, 16)
            sp.dma_start(vec[:, :], vectors).then_inc(vec_loaded, 16)
            for i, (a, b) in enumerate(CHUNKS):
                sp.dma_start(raw(a, b), weights[:, a:b]).then_inc(w_loaded[i], 16)
                if i == 0:
                    for n in range(3):
                        sp.dma_start(be_raw[n * E:(n + 1) * E, :], be).then_inc(be_loaded, 16)

            def load_x(u):
                sp.wait_ge(x_kept, u)
                sp.wait_ge(xn_ready, u)
                sp.wait_ge(nrm_ready, u)
                sp.dma_start(xb[:, :].rearrange("p (t c) -> p t c", t=TU), x_u[u]).then_inc(x_loaded, 16)
            with sp.Fori(1, NU) as u:
                load_x(u)

            with sp.Fori(0, NU - 1) as u:
                sp.wait_ge(out_ready, 2 * u + 2)
                sp.dma_start(out_u[u], z[:, u, :].rearrange("p (t c) -> p t c", t=TU)).then_inc(stored, 16)
            z_last = z[:, NU - 1, :].rearrange("p (t c) -> p t c", t=TU)
            for i in range(2):
                sp.wait_ge(out_ready, 2 * NU - 1 + i)
                half = slice(i * TU // 2, (i + 1) * TU // 2)
                sp.dma_start(out_u[NU - 1][:, half, :], z_last[:, half, :]).then_inc(stored, 16)
            sp.wait_ge(stored, 16 * (NU + 1))

        @block.tensor
        def _(pe):
            mul = nc.tensor.matmul

            def wh(col, n=P):
                return w_hi[:, col:col + n]

            def wl(col, n=P):
                return w_lo[:, col:col + n]

            def h_transposes(u):
                pe.wait_ge(nrm_ready, u + 1)
                for k in range(KC):
                    from_zero(pe, r_read, 2 * (u - 1) + k + 1)
                    for t in range(TU):
                        last = nc.tensor.transpose(ring[HT_F[k]][:, t * P:(t + 1) * P],
                                                   nrm[:, t * C + k * P:t * C + (k + 1) * P], ident)
                    last.then_inc(hT_done, 1)

            def xn_transposes(u):
                pe.wait_ge(xn_ready, u + 1)
                for k in range(KC):
                    if not (isinstance(u, int) and u == 0):
                        pe.wait_ge(kv_read, 4 * u + k + 1)
                    for t in range(TU):
                        last = nc.tensor.transpose(ring[XN_F[k]][:, t * P:(t + 1) * P],
                                                   xn[:, t * C + k * P:t * C + (k + 1) * P], ident)
                    last.then_inc(xnT_done, 1)

            def project(u, ps, i):
                for k in range(KC):
                    col = KVR0 + k * 3 * C + i * P
                    mul(ps[:, :], wh(col), xx_hi[:, k, :], start=(k == 0), stop=False)
                    mul(ps[:, :], wh(col), xx_lo[:, k, :], start=False, stop=False)
                    last = mul(ps[:, :], wl(col), xx_hi[:, k, :], start=False, stop=(k == KC - 1))
                return last

            def project_kv(u, i):
                if i == 0:
                    pe.wait_ge(xx_lo_ready, u + 1)
                    pe.wait_ge(xx_hi_ready, u + 1)
                if i < 2 and isinstance(u, int) and u == 0:
                    pe.wait_ge(xnT_lo_ready, i + 1)
                elif i < 2:
                    pe.wait_ge(acc_biased, 2 * (u - 1) + i + 1)
                elif isinstance(u, int) and u <= 1:
                    pe.wait_ge(h_ready, 2 * u + i - 1)
                else:
                    pe.wait_ge(h2_ready, 2 * (u - 2) + i - 1)
                project(u, ring[KV_F[i]], i).then_inc(kv_done, 1)

            def project_r(u, i):
                pe.wait_ge(kv_read, 4 * u + 3 + i)
                project(u, ring[R_F[i]], 4 + i).then_inc(r_done, 1)

            def logits(u):
                pe.wait_ge(xnT_lo_ready, 2 * u + 2)
                pe.wait_ge(xnT_hi_ready, 2 * u + 2)
                from_zero(pe, gT_ready, u)
                for k in range(KC):
                    col = WG0 + k * E
                    mul(logit_bank[0:E, :], wh(col, E), xnT_hi[:, k, :], start=(k == 0), stop=False)
                    mul(logit_bank[0:E, :], wl(col, E), xnT_hi[:, k, :], start=False, stop=False)
                    last = mul(logit_bank[0:E, :], wh(col, E), xnT_lo[:, k, :], start=False, stop=(k == KC - 1))
                last.then_inc(logits_done, 1)

            def logit_transposes(u):
                stand_alone(pe, (lgT_ready, u + 1))
                for t in range(TU):
                    last = nc.tensor.transpose(logit_bank[:, t * E:(t + 1) * E],
                                               lgT[:, t * P:(t + 1) * P], ident[0:E, 0:E])
                last.then_inc(logits_turned, 1)

            def y_transposes(u):
                pe.wait_ge(y_ready, u + 1)
                for i in range(2):
                    if isinstance(u, int) and u == NU - 1:
                        pe.wait_ge(acc_biased, 2 * u + i + 1)
                    else:
                        pe.wait_ge(xnT_lo_ready, 2 * (u + 1) + i + 1)
                    for t in (2 * i, 2 * i + 1):
                        for k in range(KC):
                            at = (t % 2) * C + k * P
                            last = nc.tensor.transpose(ring[YT_F[i]][:, at:at + P],
                                                       ep[:, 0, k, t * P:(t + 1) * P], ident)
                    last.then_inc(yT_done, 1)

            def h2_transposes(u):
                pe.wait_ge(nrm2_ready, u + 1)
                for k in range(KC):
                    if isinstance(u, int) and u == NU - 1:
                        pe.wait_ge(h2_ready, 2 * (u - 1) + k + 1)
                    elif isinstance(u, int) and u == NU - 2:
                        pe.wait_ge(r_read, 2 * (u + 1) + k + 1)
                    else:
                        pe.wait_ge(h_ready, 2 * (u + 2) + k + 1)
                    for t in range(TU):
                        last = nc.tensor.transpose(ring[H2_F[k]][:, t * P:(t + 1) * P],
                                                   nrm2[:, t * C + k * P:t * C + (k + 1) * P], ident)
                    last.then_inc(h2T_done, 1)

            def gate_transposes(u):
                pe.wait_ge(gates_ready, u + 1)
                for t in range(TU):
                    last = nc.tensor.transpose(gT_bank[0:3 * E, t * P:(t + 1) * P], gate3[:, t, :], ident)
                last.then_inc(gT_done, 1)

            def gate_bias(u, first):
                pe.wait_ge(gT_ready, u + 1)
                for i, tiles in enumerate(((2, 3), (0, 1))):
                    if first:
                        pe.wait_ge(xnT_lo_ready, 2 * u + i + 1)
                    else:
                        pe.wait_ge(x1_ready, 2 * (u - 1) + i + 1)
                    for t in tiles:
                        mm_last = mul(ring[BIAS_F[i]][:, (t % 2) * C:(t % 2 + 1) * C],
                                      gT3[:, t * P:(t + 1) * P], be3[:, :], start=True, stop=True)
                    mm_last.then_inc(bias_done, 1)

            def experts(u, f):
                t, q = 2 * (f // 8) + f % 2, f // 2 % Q
                from_zero(pe, moe_added, 32 * u + (added_by(f - 3) if f >= 3 else 0))
                ps = moe_bank[f % 3]
                ts = slice(t * P, (t + 1) * P)
                for k in range(KC):
                    col = WE0 + k * E * C + q * 2 * C
                    mul(ps[:, :], xnT_hi[:, k, ts], wh(col, 2 * C), start=(k == 0), stop=False)
                    mul(ps[:, :], xnT_hi[:, k, ts], wl(col, 2 * C), start=False, stop=False)
                    last = mul(ps[:, :], xnT_lo[:, k, ts], wh(col, 2 * C), start=False, stop=(k == KC - 1))
                last.then_inc(moe_done, 1)

            def step(u, first=False, last=False):
                if not first:
                    xn_transposes(u)
                project_r(u, 0)
                project_r(u, 1)
                if not first:
                    logits(u)
                if not first:
                    y_transposes(u - 1)
                if first:
                    pe.wait_ge(hi_split, SPLIT[2])
                    pe.wait_ge(lo_split, SPLIT[2])
                    pe.wait_ge(be_ready, 1)
                if not first:
                    logit_transposes(u)
                for f in range(TU * Q):
                    if f in (9, 11, 13, 15) and not last:
                        project_kv(u + 1, (f - 9) // 2)
                    experts(u, f)
                    if f == 2:
                        if not last:
                            h_transposes(u + 1)
                        gate_transposes(u)
                    if f == 4:
                        gate_bias(u, first)
                    if f == 10 and not first:
                        h2_transposes(u - 1)

            pe.wait_ge(vec_loaded, 16)
            h_transposes(0)
            xn_transposes(0)
            pe.wait_ge(hi_split, SPLIT[0])
            pe.wait_ge(lo_split, SPLIT[0])
            logits(0)
            for i in range(4):
                project_kv(0, i)
            logit_transposes(0)
            step(0, first=True)
            with pe.Fori(1, NU - 1) as u:
                step(u)
            step(NU - 1, last=True)

            x2_hi, x2_lo = (xx_hi, xnT_hi), (xx_lo, xnT_lo)

            def hidden(u, par, j):
                if j == 0:
                    pe.wait_ge(x2_lo_ready, u + 1)
                    pe.wait_ge(x2_hi_ready, u + 1)
                from_zero(pe, relu_ready, HB * u + j - 1)
                if isinstance(u, int) and u == 0 and j < 2:
                    pe.wait_ge(moe_added, 32 * (NU - 1) + added_by((TU * Q - 3, TU * Q - 1)[j]))
                ps = kc_bank[j % 2]
                for k in range(KC):
                    col = WCK0 + k * HID + j * P
                    mul(ps[:, :], wh(col), x2_hi[par][:, k, :], start=(k == 0), stop=False)
                    mul(ps[:, :], wh(col), x2_lo[par][:, k, :], start=False, stop=False)
                    last = mul(ps[:, :], wl(col), x2_hi[par][:, k, :], start=False, stop=(k == KC - 1))
                last.then_inc(kc_done, 1)

            def receptance(u, par, i):
                from_zero(pe, rc_ready, 2 * u + i - 1)
                if isinstance(u, int) and u == 0:
                    pe.wait_ge(h2_ready, 2 * NU)
                for t in (2 * i, 2 * i + 1):
                    ps = rc_bank[i][:, (t % 2) * C:(t % 2 + 1) * C]
                    ts = slice(t * P, (t + 1) * P)
                    for k in range(KC):
                        col = WCR0 + k * C
                        mul(ps, x2_hi[par][:, k, ts], wh(col, C), start=(k == 0), stop=False)
                        mul(ps, x2_hi[par][:, k, ts], wl(col, C), start=False, stop=False)
                        last = mul(ps, x2_lo[par][:, k, ts], wh(col, C), start=False, stop=(k == KC - 1))
                last.then_inc(rc_done, 1)

            def values(u, par, j):
                pe.wait_ge(sq_lo_ready, HB * u + j + 1)
                pe.wait_ge(sq_hi_ready, HB * u + j + 1)
                if j == 0:
                    from_zero(pe, rv_ready, 2 * (u - 1))
                hi, lo = sq_hi[:, j % 4, :], sq_lo[:, j % 4, :]
                for t in range(TU):
                    ps = out_bank[par][t // 2][:, (t % 2) * C:(t % 2 + 1) * C]
                    ts = slice(t * P, (t + 1) * P)
                    col = slice(j * C, (j + 1) * C)
                    mul(ps, hi[:, ts], wcv_hi[:, col], start=(j == 0 and t % 2 == 0), stop=False,
                        skip_group_check=True)
                    mul(ps, hi[:, ts], wcv_lo[:, col], start=False, stop=False, skip_group_check=True)
                    last = mul(ps, lo[:, ts], wcv_hi[:, col], start=False, stop=(j == HB - 1),
                               skip_group_check=True)
                last.then_inc(vv_done, 1)

            def mix(u, par, first=False):
                for j in range(HB):
                    hidden(u, par, j)
                    if j >= 2:
                        values(u, par, j - 2)
                    if first and j == 1:
                        y_transposes(NU - 1)
                    if first and j == 6:
                        h2_transposes(NU - 1)
                receptance(u, par, 0)
                values(u, par, HB - 2)
                receptance(u, par, 1)
                values(u, par, HB - 1)

            pe.wait_ge(hi_split, SPLIT[4])
            pe.wait_ge(lo_split, LO_SPLIT)
            pe.wait_ge(lo_split_3, N_SPLIT[3])
            mix(0, 0, first=True)
            mix(1, 1)
            with pe.Fori(1, NU // 2) as i:
                mix(2 * i, 0)
                mix(2 * i + 1, 1)

        @block.scalar
        def _(act):
            act_fn = nc.scalar.activation

            def split_hi(i):
                act.wait_ge(w_loaded[i], 16)
                for hi, _, src in parts(*CHUNKS[i]):
                    act_fn(hi, src, ACT.Copy).then_inc(hi_split, 1)

            def h_read(u):
                act.wait_ge(h_first, u + 1)
                for k in range(KC):
                    act.wait_ge(hT_done, 2 * u + k + 1)
                    act_fn(h[:, k, 1:U + 1], ring[HT_F[k]][:, :], ACT.Identity,
                           bias=v(V_LN1B, k), scale=v(V_LN1W, k)).then_inc(h_ready, 1)

            def xx_split(u):
                act.wait_ge(xxx_ready, 2 * u + 2)
                from_zero(act, r_done, 2 * u)
                act_fn(xx_hi[:, :, :], xxx, ACT.Copy).then_inc(xx_hi_ready, 1)

            def xn_read(u):
                for k in range(KC):
                    act.wait_ge(xnT_done, 2 * u + k + 1)
                    act_fn(xnT_hi[:, k, :], ring[XN_F[k]][:, :], ACT.Copy).then_inc(xnT_hi_ready, 1)

            def kv_out(u, i):
                act.wait_ge(kv_done, 4 * u + i + 1)
                if i == 0:
                    from_zero(act, sg_ready, 2 * u)
                if i == 2:
                    from_zero(act, v_used, u)
                act_fn((kg, vv)[i // 2][:, i % 2, :], ring[KV_F[i]][:, :], ACT.Copy).then_inc(kv_read, 1)

            def r_out(u, i):
                act.wait_ge(r_done, 2 * u + i + 1)
                from_zero(act, y_ready, u)
                act_fn(rr[:, i, :], ring[R_F[i]][:, :], ACT.Sigmoid).then_inc(r_read, 1)

            def lgT_read(u):
                act.wait_ge(logits_done, u + 1)
                if not (isinstance(u, int) and u == 0):
                    act.wait_ge(wkv_own, 4 * u + 3)
                act_fn(lgT, logit_bank[0:E, :], ACT.Identity, bias=vec[0:E, V_BG:V_BG + 1]).then_inc(lgT_ready, 1)

            def top_exp(u):
                act.wait_ge(dif_ready, u + 1)
                act_fn(ex[:, :], dif[:, :], ACT.Exp, scale=-1.0).then_inc(ex_ready, 1)

            def gT_read(u):
                act.wait_ge(gT_done, u + 1)
                act.wait_ge(r_done, 2 * u + 2)
                act_fn(gT3, gT_bank[0:3 * E, :], ACT.Copy).then_inc(gT_ready, 1)

            def exp_g(u, i):
                act.wait_ge(relu_g_ready, 2 * u + 2 - i)
                act_fn(ep[:, i], ep[:, i], ACT.Exp, scale=-1.0).then_inc(eg_ready, 1)

            def relu_g(u, i):
                act.wait_ge(g_ready, u + 1)
                if i == 0:
                    from_zero(act, yT_done, 2 * u)
                else:
                    from_zero(act, y_own, 2 * u - 1)
                act_fn(ep[:, i], kg[:, :, :], ACT.Relu, scale=(-1.0, 1.0)[i]).then_inc(relu_g_ready, 1)

            def ln_s(u):
                act.wait_ge(s_ready, u + 1)
                act_fn(sl[:, :, 1:U + 1], sl[:, :, 1:U + 1], ACT.Ln).then_inc(ln_ready, 1)

            def exp_d(u):
                act.wait_ge(d_ready, u + 1)
                act_fn(ep[:, 0], kg[:, :, :], ACT.Exp).then_inc(ed_ready, 1)
                act_fn(ep[:, 1], kg[:, :, :], ACT.Exp, scale=-1.0).then_inc(ed_ready, 1)

            def sigmoid_d(u):
                act.wait_ge(aa_ready, 2 * u + 2)
                for k in range(KC):
                    act_fn(ep[:, 1, k, :], kg[:, k, :], ACT.Sigmoid, bias=v(V_U, k)).then_inc(sg_ready, 1)

            def h2_read(u):
                act.wait_ge(lo_split, LO_SPLIT)
                act.wait_ge(lo_split_3, N_SPLIT[3])
                for k in range(KC):
                    act.wait_ge(h2T_done, 2 * u + k + 1)
                    act_fn(h2[:, k, u * U:(u + 1) * U] if isinstance(u, int) else h2[:, k, bass.ds(u * U, U)],
                           ring[H2_F[k]][:, :], ACT.Identity,
                           bias=v(V_LN2B, k), scale=v(V_LN2W, k)).then_inc(h2_ready, 1)

            def ln2_norm(u):
                stand_alone(act, (nb3_ready, u + 1))
                for t in range(TU):
                    last = act_fn(nrm2[:, t * C:(t + 1) * C], z[:, u, t * C:(t + 1) * C], ACT.Identity,
                                  bias=nb3[:, t:t + 1], scale=r3[:, t:t + 1])
                last.then_inc(nrm2_ready, 1)

            def x2_split(u, par):
                act.wait_ge(x2_own, 3 * KC * (u + 1))
                if isinstance(u, int) and u < 2:
                    act.wait_ge((r_done, moe_done)[u], (2 * NU, TU * Q * NU)[u])
                from_zero(act, kc_done, HB * (u - 1))
                from_zero(act, rc_done, 2 * (u - 1))
                act_fn((xx_hi, xnT_hi)[par][:, :, :], xxx, ACT.Copy).then_inc(x2_hi_ready, 1)

            def copy_xn(u):
                stand_alone(act, (xn_ready, u + 1))
                act_fn(z[:, u, :], xn[:, :], ACT.Copy).then_inc(z_copied, 1)

            def keep_x(u, par):
                act.wait_ge(x_loaded, 16 * (u + 1))
                from_zero(act, z_ready, u - 1)
                act_fn(acc[:, par, :], xb[:, :], ACT.Copy).then_inc(x_kept, 1)

            def step(u, par, first=False, last=False):
                if not first:
                    xn_read(u)
                    lgT_read(u)
                r_out(u, 0)
                r_out(u, 1)
                nc.scalar.preload_act_table_set("natural_log_exp_and_others")
                top_exp(u)
                relu_g(u, 1)
                exp_g(u, 1)
                relu_g(u, 0)
                if not last:
                    h_read(u + 1)
                exp_g(u, 0)
                gT_read(u)
                if last:
                    x2_split(0, 0)
                else:
                    xx_split(u + 1)
                if first:
                    split_hi(3)
                    split_hi(4)
                ln_s(u)
                if not first:
                    ln2_norm(u - 1)
                exp_d(u)
                if not last:
                    keep_x(u + 1, 1 - par)
                    copy_xn(u + 1)
                if not first:
                    h2_read(u - 1)
                sigmoid_d(u)
                if not last:
                    for i in range(4):
                        kv_out(u + 1, i)

            act.wait_ge(vec_loaded, 16)
            keep_x(0, 0)
            split_hi(0)
            h_read(0)
            xn_read(0)
            xx_split(0)
            split_hi(1)
            act.wait_ge(be_loaded, 3 * 16)
            act_fn(be3[:, :], be_raw, ACT.Identity, bias=0.0,
                   scale=vec[0:3 * E, V_BE_G:V_BE_G + 1]).then_inc(be_hi_ready, 1)
            copy_xn(0)
            lgT_read(0)
            split_hi(2)
            for i in range(4):
                kv_out(0, i)
            step(0, 0, first=True)
            with act.Fori(0, (NU - 2) // 2) as i:
                step(2 * i + 1, 1)
                step(2 * i + 2, 0)
            step(NU - 1, 1, last=True)

            def mix(u, par, first=False, last=False):
                for j in range(HB):
                    if first and j == 3:
                        ln2_norm(NU - 1)
                    if first and j == 7:
                        h2_read(NU - 1)
                    act.wait_ge(kc_done, HB * u + j + 1)
                    from_zero(act, sq_ready, HB * u + j - 1)
                    act_fn(relu[:, j % 2, :], kc_bank[j % 2][:, :], ACT.Relu).then_inc(relu_ready, 1)
                    act.wait_ge(relu_ready, HB * u + j + 1)
                    from_zero(act, sq_lo_ready, HB * u + j - 1)
                    from_zero(act, sq_hi_ready, HB * u + j - 1)
                    act_fn(sq[:, j % 2, :], relu[:, j % 2, :], ACT.Square).then_inc(sq_ready, 1)
                    if j == 4 and not last:
                        x2_split(u + 1, 1 - par)
                for i in range(2):
                    act.wait_ge(rc_done, 2 * u + i + 1)
                    from_zero(act, out_ready, 2 * u + i - 1)
                    act_fn(rc[:, i * 2 * C:(i + 1) * 2 * C], rc_bank[i][:, :],
                           ACT.Sigmoid).then_inc(rc_ready, 1)

            act.wait_ge(z_ready, NU - 1)
            act.wait_ge(xn_ready, NU)
            act.wait_ge(nrm_ready, NU)
            mix(0, 0, first=True)
            mix(1, 1)
            with act.Fori(1, NU // 2 - 1) as i:
                mix(2 * i, 0)
                mix(2 * i + 1, 1)
            mix(NU - 2, 0)
            mix(NU - 1, 1, last=True)

        @block.vector
        def _(dve):
            tt, ts_, stt = nc.vector.tensor_tensor, nc.vector.tensor_scalar, nc.vector.scalar_tensor_tensor
            scan = nc.vector.tensor_tensor_scan
            copy = nc.vector.tensor_copy

            def tile(buf, t, n=1):
                return buf[:, t * C:(t + n) * C]

            def split_lo(i):
                dve.wait_ge(hi_split, SPLIT[i])
                for hi, lo, src in parts(*CHUNKS[i]):
                    tt(lo, src, hi, ALU.subtract).then_inc(lo_split, 1)

            def ln1_stats(u):
                dve.wait_ge(x_loaded, 16 * (u + 1))
                for t in range(TU):
                    nc.vector.bn_stats(st1[:, t, :], tile(xb, t)).then_inc(ln1_own, 1)

            def ln1_variances(u):
                stand_alone(dve, (ln1_own, 8 * u + 4))
                for t in range(TU):
                    nc.vector.bn_aggr(mv1[:, t, :], st1[:, t, :]).then_inc(ln1_own, 1)
                dve.wait_ge(ln1_own, 8 * u + 8)
                ts_(ve1[:, 0, :], mv1[:, :, 1], EPS, None, ALU.add).then_inc(ve1_ready, 1)
                ts_(ve1[:, 1, :], mv1[:, :, 1], 1.0 + EPS, EPS * EPS, ALU.mult, ALU.add).then_inc(ve1_ready, 1)

            def ln1_coefficients(u):
                dve.wait_ge(r1_ready, u + 1)
                for n in range(2):
                    stt(nb1[:, n, :], mv1[:, :, 0], -1.0, r1[:, n, :], ALU.mult, ALU.mult).then_inc(nb1_ready, 1)

            def h_column(start):
                if start:
                    copy(h[:, :, 0], vec[:, V_TS:V_TS + KC]).then_inc(h_first, 1)
                else:
                    copy(h[:, :, 0], h[:, :, U]).then_inc(h_first, 1)

            def xxx_mix(u, next_starts, last=False):
                for k in range(KC):
                    dve.wait_ge(a_ready, 2 * u + k + 1)
                    stt(xxx[:, k, :], h[:, k, 0:U], tsd[:, 1, k:k + 1], xxx[:, k, :],
                        ALU.mult, ALU.add).then_inc(xxx_ready, 1)
                if not last:
                    dve.wait_ge(xxx_ready, 2 * u + 2)
                    h_column(next_starts)

            def x2_mix(u, half):
                if isinstance(u, int) and u == 0:
                    dve.wait_ge(xx_hi_ready, NU)
                    dve.wait_ge(xx_lo_ready, NU)
                dve.wait_ge(h2_ready, 2 * min(u + 2, NU) if isinstance(u, int) else 2 * NU)
                from_zero(dve, x2_hi_ready, u)
                from_zero(dve, x2_lo_ready, u)
                for k in range(KC):
                    ts_(xxx[:, k, :], h2[:, k, bass.ds(u * U, U)], tsd[:, 2, k:k + 1], None,
                        ALU.mult).then_inc(x2_own, 1)
                for k in range(KC):
                    dve.wait_ge(x2_own, 3 * KC * u + k + 1)
                    ts_k = v(V_TS, k)
                    if half == 0:
                        stt(xxx[:, k, 1:U], h2[:, k, bass.ds(u * U, U - 1)], ts_k, xxx[:, k, 1:U],
                            ALU.mult, ALU.add).then_inc(x2_own, 1)
                        stt(xxx[:, k, 0:1], h2[:, k, bass.ds(u * U + T - 1, 1)], ts_k, xxx[:, k, 0:1],
                            ALU.mult, ALU.add).then_inc(x2_own, 1)
                    else:
                        stt(xxx[:, k, :], h2[:, k, bass.ds(u * U - 1, U)], ts_k, xxx[:, k, :],
                            ALU.mult, ALU.add).then_inc(x2_own, 2)

            def xn_low(u):
                for k in range(KC):
                    dve.wait_ge(xnT_hi_ready, 2 * u + k + 1)
                    tt(xnT_lo[:, k, :], ring[XN_F[k]][:, :], xnT_hi[:, k, :],
                       ALU.subtract).then_inc(xnT_lo_ready, 1)

            gate_parts = gate3[:, :, :].rearrange("p t (s e) -> p t s e", s=3)

            def choose_experts(u):
                dve.wait_ge(logits_turned, u + 1)
                copy(lg[:, :, :], logit_bank[:, 0:TU * E].rearrange("p (t e) -> p t e", t=TU)).then_inc(
                    logits_read, 1)
                stand_alone(dve, (logits_read, u + 1))
                for t in range(TU):
                    nc.vector.max(top[:, t, :], lg[:, t, :]).then_inc(gates_own, 1)
                dve.wait_ge(gates_own, 14 * u + 4)
                tt(dif[:, :], top[:, :, 0], top[:, :, 1], ALU.subtract).then_inc(dif_ready, 1)
                for t in range(TU):
                    nc.vector.max_index(idx[:, t, :], top[:, t, :], lg[:, t, :]).then_inc(gates_own, 1)
                dve.wait_ge(gates_own, 14 * u + 8)
                copy(idxf[:, :, :], idx[:, :, 0:2]).then_inc(gates_own, 1)
                dve.wait_ge(gates_own, 14 * u + 9)
                for n in range(2):
                    tt(hot[n][:, :, :], iota, idxf[:, :, n:n + 1].to_broadcast([P, TU, E]),
                       ALU.is_equal).then_inc(gates_own, 1)

            def weigh_experts(u):
                dve.wait_ge(ex_ready, u + 1)
                ts_(tw[:, 0, :], ex[:, :], 1.0, None, ALU.add).then_inc(tw_own, 1)
                dve.wait_ge(tw_own, 3 * u + 1)
                nc.vector.reciprocal(tw[:, 0, :], tw[:, 0, :]).then_inc(tw_own, 1)
                dve.wait_ge(tw_own, 3 * u + 2)
                tt(tw[:, 1, :], ex[:, :], tw[:, 0, :], ALU.mult).then_inc(tw_own, 1)
                dve.wait_ge(tw_own, 3 * u + 3)
                dve.wait_ge(gates_own, 14 * u + 11)
                for n in range(2):
                    tt(hot[n][:, :, :], hot[n][:, :, :], tw[:, n, :].unsqueeze(2).to_broadcast([P, TU, E]),
                       ALU.mult).then_inc(gates_own, 1)
                dve.wait_ge(gates_own, 14 * u + 13)
                from_zero(dve, gT_done, u)
                tt(gate_parts[:, :, 0:3:2, :], hot[0][:, :, :].unsqueeze(2).to_broadcast([P, TU, 2, E]),
                   hot[1][:, :, :].unsqueeze(2).to_broadcast([P, TU, 2, E]), ALU.add).then_inc(gates_own, 1)
                dve.wait_ge(gates_own, 14 * u + 14)
                copy(gate_hi[:, :, :], gate).then_inc(gate_hi_ready, 1)

            def split_gates(u):
                dve.wait_ge(gate_hi_ready, u + 1)
                tt(gate_parts[:, :, 1, :], gate, gate_hi[:, :, :], ALU.subtract).then_inc(gates_ready, 1)

            def add_bias(u, par, i):
                dve.wait_ge(bias_done, 2 * u + i + 1)
                dve.wait_ge(x_kept, u + 1)
                if i == 1:
                    dve.wait_ge(moe_added, 32 * u + 16)
                a = acc[:, par, 2 * (1 - i) * C:2 * (2 - i) * C]
                tt(a, a, ring[BIAS_F[i]][:, :], ALU.add).then_inc(acc_biased, 1)

            def add_expert(u, par, i):
                f, n = 2 * (i // 4) + i % 2, i % 4 // 2
                t, q = 2 * (f // 8) + f % 2, f // 2 % Q
                if i == 0:
                    dve.wait_ge(x_kept, u + 1)
                    dve.wait_ge(gates_own, 14 * u + 14)
                if i == 16:
                    dve.wait_ge(acc_biased, 2 * u + 1)
                if n == 0:
                    dve.wait_ge(moe_done, TU * Q * u + f + 1)
                from_zero(dve, moe_added, 32 * u + i - 1)
                a = tile(acc[:, par], t)
                stt(a, moe_bank[f % 3][:, n * C:(n + 1) * C], gate[:, t, 2 * q + n:2 * q + n + 1], a,
                    ALU.mult, ALU.add).then_inc(moe_added, 1)

            def add_y(u):
                dve.wait_ge(z_copied, u + 1)
                for i in range(2):
                    dve.wait_ge(yT_done, 2 * u + i + 1)
                    zi = z[:, u, 2 * i * C:2 * (i + 1) * C]
                    tt(zi, zi, ring[YT_F[i]][:, :], ALU.add).then_inc(x1_ready, 1)

            def ln2_stats(u):
                stand_alone(dve, (x1_ready, 2 * u + 2))
                for t in range(TU):
                    nc.vector.bn_stats(st2[:, t, :], z[:, u, t * C:(t + 1) * C]).then_inc(ln2_own, 1)

            def ln2_variances(u):
                stand_alone(dve, (ln2_own, 8 * u + 4))
                for t in range(TU):
                    nc.vector.bn_aggr(mv2[:, t, :], st2[:, t, :]).then_inc(ln2_own, 1)
                dve.wait_ge(ln2_own, 8 * u + 8)
                ts_(ve3[:, :], mv2[:, :, 1], EPS, None, ALU.add).then_inc(ve3_ready, 1)

            def ln2_coefficients(u):
                dve.wait_ge(r3_ready, u + 1)
                stt(nb3[:, :], mv2[:, :, 0], -1.0, r3[:, :], ALU.mult, ALU.mult).then_inc(nb3_ready, 1)

            def wkv_max(u, start):
                from_zero(dve, g_ready, u)
                if start:
                    nc.vector.memset(mm[:, :, 0], 0.0).then_inc(wkv_own, 1)
                else:
                    copy(mm[:, :, 0], mm[:, :, U]).then_inc(wkv_own, 1)
                dve.wait_ge(wkv_own, 4 * u + 1)
                for k in range(KC):
                    dve.wait_ge(kv_read, 4 * u + k + 1)
                    scan(mm[:, k, 1:U + 1], kg[:, k, :], zero1[:, 0:1].to_broadcast([P, U]),
                         mm[:, k, 0:1], ALU.max, ALU.max).then_inc(m_ready, 1)

            def wkv_carry(u, start):
                from_zero(dve, d_ready, u)
                if start:
                    nc.vector.memset(sl[:, :, 0], 0.0).then_inc(wkv_own, 1)
                    nc.vector.memset(s_last[:, :], 1.0).then_inc(wkv_own, 1)
                else:
                    copy(sl[:, :, 0], sl[:, :, U]).then_inc(wkv_own, 2)
            def wkv_sum(u):
                dve.wait_ge(wkv_own, 4 * u + 3)
                dve.wait_ge(eg_ready, 2 * u + 2)
                dve.wait_ge(logits_turned, u + 1)
                for k in range(KC):
                    scan(sl[:, k, 1:U + 1], ep[:, 1, k, :], ep[:, 0, k, :], s_last[:, k:k + 1],
                         ALU.mult, ALU.add).then_inc(m_ready, 1)
                dve.wait_ge(m_ready, 4 * u + 4)
                copy(s_last[:, :], sl[:, :, U]).then_inc(s_ready, 1)

            def wkv_clip_a(u, start):
                dve.wait_ge(ed_ready, 2 * u + 2)
                ts_(ep[:, 1], ep[:, 1], 1.0, None, ALU.min).then_inc(ep_own, 1)
                from_zero(dve, y_ready, u)
                if start:
                    nc.vector.memset(aa[:, :, 0], 0.0).then_inc(wkv_own, 1)
                else:
                    copy(aa[:, :, 0], aa[:, :, U]).then_inc(wkv_own, 1)

            def wkv_cv(u):
                dve.wait_ge(kv_read, 4 * u + 4)
                stt(ep[:, 0], ep[:, 0], 1.0, vv[:, :, :], ALU.min, ALU.mult).then_inc(ep_own, 1)

            def wkv_aa(u):
                dve.wait_ge(ep_own, 2 * u + 2)
                dve.wait_ge(wkv_own, 4 * u + 4)
                for k in range(KC):
                    scan(aa[:, k, 1:U + 1], ep[:, 1, k, :], ep[:, 0, k, :], aa[:, k, 0:1],
                         ALU.mult, ALU.add).then_inc(aa_ready, 1)

            def step(u, par, start, first=False, last=False, second_last=False):
                def add(a, b):
                    for i in range(a, b):
                        add_expert(u, par, i)
                if not first:
                    xn_low(u)
                wkv_max(u, start)
                wkv_carry(u, start)
                if not first:
                    add_y(u - 1)
                choose_experts(u)
                weigh_experts(u)
                add(0, 1)
                split_gates(u)
                add(1, 4)
                if not first:
                    ln2_stats(u - 1)
                add(4, 7)
                if last:
                    x2_mix(0, 0)
                else:
                    xxx_mix(u + 1, next_starts=start, last=second_last)
                add(7, 10)
                if not first:
                    ln2_variances(u - 1)
                add(10, 12)
                wkv_sum(u)
                add(12, 14)
                if not first:
                    ln2_coefficients(u - 1)
                add_bias(u, par, 0)
                add(14, 17)
                add_bias(u, par, 1)
                add(17, 18)
                wkv_clip_a(u, start)
                add(18, 19)
                wkv_cv(u)
                add(19, 21)
                wkv_aa(u)
                add(21, 25)
                if first:
                    split_lo(4)
                if not last and not second_last:
                    ln1_stats(u + 2)
                add(25, 27)
                if not last and not second_last:
                    ln1_variances(u + 2)
                add(27, 29)
                if not last and not second_last:
                    ln1_coefficients(u + 2)
                add(29, 32)

            nc.vector.memset(zero1[:, :], 0.0).then_inc(zero_ready, 1)
            nc.vector.memset(half_neg[:, :, :], -0.5).then_inc(consts_ready, 1)
            ln1_stats(0)
            ln1_variances(0)
            ts_row = vec[:, V_TS:V_TS + KC]
            ts_(tsd[:, 0, :], ts_row, 1.0, None, ALU.add).then_inc(ts_ready, 1)
            ts_(tsd[:, 1, :], ts_row, -1.0, None, ALU.mult).then_inc(ts_ready, 1)
            ts_(tsd[:, 2, :], ts_row, -1.0, 1.0, ALU.mult, ALU.add).then_inc(ts_ready, 1)
            h_column(True)
            ln1_coefficients(0)
            split_lo(0)
            dve.wait_ge(ts_ready, 3)
            dve.wait_ge(zero_ready, 1)
            xxx_mix(0, next_starts=False)
            xn_low(0)
            dve.wait_ge(xx_hi_ready, 1)
            tt(xx_lo[:, :, :], xxx, xx_hi[:, :, :], ALU.subtract).then_inc(xx_lo_ready, 1)
            split_lo(1)
            split_lo(2)
            dve.wait_ge(be_hi_ready, 1)
            stt(be3[:, :], be_raw, vec[0:3 * E, V_BE_S:V_BE_S + 1], be3[:, :],
                ALU.mult, ALU.add).then_inc(be_ready, 1)
            ln1_stats(1)
            ln1_variances(1)
            ln1_coefficients(1)
            step(0, 0, True, first=True)
            with dve.Fori(0, (NU - 4) // 2) as i:
                step(2 * i + 1, 1, False)
                step(2 * i + 2, 0, True)
            step(NU - 3, 1, False)
            step(NU - 2, 0, True, second_last=True)
            step(NU - 1, 1, False, last=True)

            x2_hi, x2_lo = (xx_hi, xnT_hi), (xx_lo, xnT_lo)

            def x2_low(u, par):
                dve.wait_ge(x2_hi_ready, u + 1)
                tt(x2_lo[par][:, :, :], xxx, x2_hi[par][:, :, :], ALU.subtract).then_inc(x2_lo_ready, 1)

            def squares(u, j):
                dve.wait_ge(sq_ready, HB * u + j + 1)
                from_zero(dve, vv_done, HB * u + j - 3)
                copy(sq_hi[:, j % 4, :], sq[:, j % 2, :]).then_inc(sq_hi_ready, 1)
                dve.wait_ge(sq_hi_ready, HB * u + j + 1)
                tt(sq_lo[:, j % 4, :], sq[:, j % 2, :], sq_hi[:, j % 4, :], ALU.subtract).then_inc(sq_lo_ready, 1)

            def finish(u, par):
                dve.wait_ge(vv_done, HB * u + HB)
                for i in range(2):
                    dve.wait_ge(rc_ready, 2 * u + i + 1)
                    r_i = tile(rc, 2 * i, 2)
                    tt(r_i, out_bank[par][i][:, :], r_i, ALU.mult).then_inc(rv_ready, 1)

            def mix(u, par, first=False, last=False):
                for j in range(HB):
                    squares(u, j)
                    if first and j == 0:
                        add_y(NU - 1)
                        ln2_stats(NU - 1)
                        ln2_variances(NU - 1)
                    if first and j == 1:
                        ln2_coefficients(NU - 1)
                    if j == 2 and not last:
                        x2_mix(u + 1, 1 - par)
                    if j == 5 and not last:
                        x2_low(u + 1, 1 - par)
                finish(u, par)

            mix(0, 0, first=True)
            mix(1, 1)
            with dve.Fori(1, NU // 2 - 1) as i:
                mix(2 * i, 0)
                mix(2 * i + 1, 1)
            mix(NU - 2, 0)
            mix(NU - 1, 1, last=True)

        @block.gpsimd
        def _(pool):
            tt, ts_ = nc.gpsimd.tensor_tensor, nc.gpsimd.tensor_scalar

            def tile(buf, t):
                return buf[:, t * C:(t + 1) * C]

            def ln1_rstd(u):
                pool.wait_ge(ve1_ready, 2 * u + 2)
                tt(r1[:, :, :], ve1[:, :, :], half_neg[:, :, :], ALU.pow).then_inc(r1_ready, 1)

            def ln1_norm(u):
                stand_alone(pool, (nb1_ready, 2 * u + 2), (xx_lo_ready, u), (xx_hi_ready, u))
                for t in range(TU):
                    last = ts_(tile(nrm, t), tile(xb, t), r1[:, 1, t:t + 1], nb1[:, 1, t:t + 1],
                               ALU.mult, ALU.add)
                last.then_inc(nrm_ready, 1)

            def make_xn(u):
                stand_alone(pool, (xnT_done, 2 * u), (z_copied, u))
                for t in range(TU):
                    last = ts_(tile(xn, t), tile(xb, t), r1[:, 0, t:t + 1], nb1[:, 0, t:t + 1],
                               ALU.mult, ALU.add)
                last.then_inc(xn_ready, 1)

            def scale_h(u):
                for k in range(KC):
                    stand_alone(pool, (h_ready, 2 * u + k + 1), (hT_done, 2 * u + 2))
                    ts_(xxx[:, k, :], h[:, k, 1:U + 1], tsd[:, 0, k:k + 1], 0.0,
                        ALU.mult, ALU.add).then_inc(a_ready, 1)

            def make_g(u):
                pool.wait_ge(m_ready, 4 * u + 2)
                tt(kg[:, :, :], kg[:, :, :], mm[:, :, 0:U], ALU.subtract).then_inc(g_ready, 1)

            def ln2_rstd(u):
                pool.wait_ge(ve3_ready, u + 1)
                tt(r3[:, :], ve3[:, :], half_neg[:, 0, :], ALU.pow).then_inc(r3_ready, 1)

            def add_acc(u, par):
                pool.wait_ge(nrm2_ready, u + 1)
                pool.wait_ge(moe_added, 32 * (u + 1))
                tt(z[:, u, :], z[:, u, :], acc[:, par, :], ALU.add).then_inc(z_ready, 1)

            def xx_low(u):
                pool.wait_ge(xx_hi_ready, u + 1)
                from_zero(pool, bias_done, 2 * u)
                tt(xx_lo[:, :, :], xxx, xx_hi[:, :, :], ALU.subtract).then_inc(xx_lo_ready, 1)

            def finish_wkv(u, meanwhile=None):
                pool.wait_ge(aa_ready, 2 * u + 2)
                tt(ep[:, 0], vv[:, :, :], aa[:, :, 0:U], ALU.subtract).then_inc(v_used, 1)
                pool.wait_ge(v_used, u + 1)
                pool.wait_ge(sg_ready, 2 * u + 2)
                tt(ep[:, 0], ep[:, 0], ep[:, 1], ALU.mult).then_inc(y_own, 1)
                if meanwhile is not None:
                    ln1_rstd(meanwhile)
                pool.wait_ge(y_own, 2 * u + 1)
                tt(ep[:, 0], ep[:, 0], aa[:, :, 0:U], ALU.add).then_inc(y_own, 1)
                pool.wait_ge(y_own, 2 * u + 2)
                tt(ep[:, 0], ep[:, 0], rr[:, :, :], ALU.mult).then_inc(y_ready, 1)

            def split_lo_3():
                pool.wait_ge(hi_split, SPLIT[3])
                for hi, lo, src in parts(*CHUNKS[3]):
                    tt(lo, src, hi, ALU.subtract).then_inc(lo_split_3, 1)

            def make_d(u):
                pool.wait_ge(ln_ready, u + 1)
                tt(kg[:, :, :], kg[:, :, :], sl[:, :, 0:U], ALU.subtract).then_inc(d_ready, 1)

            def step(u, par, first=False, last=False, second_last=False):
                make_g(u)
                if not last:
                    if not first:
                        ln1_norm(u + 1)
                    make_xn(u + 1)
                if not last:
                    scale_h(u + 1)
                if last:
                    pool.wait_ge(bias_done, 2 * NU)
                    pool.wait_ge(x2_hi_ready, 1)
                    tt(xx_lo[:, :, :], xxx, xx_hi[:, :, :], ALU.subtract).then_inc(x2_lo_ready, 1)
                else:
                    xx_low(u + 1)
                if not first:
                    ln2_rstd(u - 1)
                make_d(u)
                if first:
                    split_lo_3()
                if not first:
                    add_acc(u - 1, 1 - par)
                finish_wkv(u, None if last or second_last else u + 2)

            pool.wait_ge(consts_ready, 1)
            ln1_rstd(0)
            ln1_norm(0)
            make_xn(0)
            pool.wait_ge(ts_ready, 3)
            scale_h(0)
            ln1_rstd(1)
            ln1_norm(1)
            step(0, 0, first=True)
            with pool.Fori(0, (NU - 4) // 2) as i:
                step(2 * i + 1, 1)
                step(2 * i + 2, 0)
            step(NU - 3, 1)
            step(NU - 2, 0, second_last=True)
            step(NU - 1, 1, last=True)
            ln2_rstd(NU - 1)
            add_acc(NU - 1, 1)

            with pool.Fori(0, NU) as u:
                for i in range(2):
                    pool.wait_ge(rv_ready, 2 * u + i + 1)
                    zi = z[:, u, 2 * i * C:2 * (i + 1) * C]
                    tt(zi, zi, rc[:, 2 * i * C:2 * (i + 1) * C], ALU.add).then_inc(out_ready, 1)


_OUT = ("out", (B, T, C))


def kernel(**inputs):
    import numpy as np
    import concourse.bacc as bacc
    from concourse import mybir as mb
    from concourse.bass_utils import run_bass_kernel_spmd

    a = {k.removeprefix("L0_"): np.asarray(val) for k, val in inputs.items()}

    def rows(w):
        n = w.shape[0] // P
        return w.reshape(n, P, w.shape[1]).transpose(1, 0, 2).reshape(P, -1)

    def column(vec):
        return vec.reshape(KC, P).T

    kvr = np.concatenate([a["attn_Wk"].T, a["attn_Wv"].T, a["attn_Wr"].T], axis=1)
    we = a["ffn_We"].transpose(1, 0, 2).reshape(C, E * C)
    weights = np.concatenate([rows(w) for w in (
        kvr, a["ffn_Wg"], we, a["attn_Wck"].T, a["attn_Wcr"].T, a["attn_Wcv"].T)], axis=1)

    vectors = np.concatenate(
        [column(a["attn_" + n]) for n in ("ln1_w", "ln1_b", "ln2_w", "ln2_b")]
        + [column(a["attn_time_shift"]), column(a["attn_time_first"]),
           np.pad(a["ffn_bg"].reshape(E, 1), ((0, P - E), (0, 0))),
           np.repeat(np.float32([[0, 1], [0, 1], [1, -1], [0, 0]]), (E, E, E, P - 3 * E), axis=0),
           np.broadcast_to(np.arange(E, dtype=np.float32), (P, E)),
           np.eye(P, dtype=np.float32)], axis=1)
    arrays = {"x": a["attn_x"], "weights": weights, "vectors": vectors, "be": a["ffn_be"]}
    arrays = {k: np.ascontiguousarray(val) for k, val in arrays.items()}

    nc = bacc.Bacc("TRN2", target_bir_lowering=False, num_devices=1, dynamic_dma_scratch_size=256)
    aps = [nc.dram_tensor(k, val.shape, mb.dt.float32, kind="ExternalInput").ap() for k, val in arrays.items()]
    aps.append(nc.dram_tensor(_OUT[0], _OUT[1], mb.dt.float32, kind="ExternalOutput").ap())
    rwkv_moe(nc, *aps)
    return run_bass_kernel_spmd(nc, [arrays], core_ids=[0]).results[0][_OUT[0]]
```
